# Optimizing a Trainium2 kernel written in Bass

```python
import numpy as np
import jax
import jax.numpy as jnp

def _softmax(x, axis=-1):
    return jax.nn.softmax(x, axis=axis)

def _gelu(x):
    return jax.nn.gelu(x, approximate=True)

def _silu(x):
    return jax.nn.silu(x)

def _sigmoid(x):
    return jax.nn.sigmoid(x)

def _layernorm(x, axis=-1, eps=1e-05):
    m = jnp.mean(x, axis=axis, keepdims=True)
    v = jnp.var(x, axis=axis, keepdims=True)
    return (x - m) / jnp.sqrt(v + eps)

def _scatter_add(tgt, idx, src, axis=0):
    return tgt.at[idx].add(src)

def _segment_sum(src, seg, n):
    return jax.ops.segment_sum(src, seg, n)
kernel_name = 'mk_gnn_preln_d1_gnn_r32_934935'

def setup_inputs(seed: int=0):
    np.random.seed(seed)
    _w = jnp.asarray

    def _rec_inputs():
        import jax
        import jax.numpy as jnp
        _gk = jax.random.key(seed)
        x = -0.0003713 + 1 * jax.random.normal(jax.random.fold_in(_gk, 1), (3125, 128), jnp.float32)
        _s = jax.random.randint(jax.random.fold_in(_gk, 2), (50000,), 0, 3125, jnp.int32)
        _d = jax.random.randint(jax.random.fold_in(_gk, 3), (50000,), 0, 3125, jnp.int32)
        _loop = jnp.arange(3125, dtype=jnp.int32)
        src = jnp.concatenate([_s, _d, _loop])
        dst = jnp.concatenate([_d, _s, _loop])
        _o = jnp.argsort(dst, stable=True)
        src = src[_o]
        dst = dst[_o]
        return (x, src, dst)
    x, src, dst = _rec_inputs()

    def _L0_gnn_setup():
        import jax, jax.numpy as jnp
        import numpy as np
        N_NODES = 3125
        N_EDGES = 18750
        H = 128
        NUM_STEPS = 5
        key = jax.random.key(seed)
        ks = jax.random.split(key, 8)
        s = 0.05
        return {'x': jax.random.normal(ks[0], (N_NODES, H), dtype=jnp.float32), 'edge_index': jax.random.randint(ks[1], (2, N_EDGES), 0, N_NODES, dtype=jnp.int64), 'W_msg': jax.random.normal(ks[2], (H, H), dtype=jnp.float32) * s, 'b_msg': jax.random.normal(ks[3], (H,), dtype=jnp.float32) * s, 'W_ih': jax.random.normal(ks[4], (3 * H, H), dtype=jnp.float32) * s, 'W_hh': jax.random.normal(ks[5], (3 * H, H), dtype=jnp.float32) * s, 'b_ih': jax.random.normal(ks[6], (3 * H,), dtype=jnp.float32) * s, 'b_hh': jax.random.normal(ks[7], (3 * H,), dtype=jnp.float32) * s}
    _L0_gnn_all = _L0_gnn_setup()
    _L0_gnn_in = {k: v for k, v in _L0_gnn_all.items() if k in ('W_msg', 'b_msg', 'W_ih', 'W_hh', 'b_ih', 'b_hh')}
    del _L0_gnn_all
    return {'x': x, 'src': src, 'dst': dst, 'L0_gnn_W_msg': _L0_gnn_in['W_msg'], 'L0_gnn_b_msg': _L0_gnn_in['b_msg'], 'L0_gnn_W_ih': _L0_gnn_in['W_ih'], 'L0_gnn_W_hh': _L0_gnn_in['W_hh'], 'L0_gnn_b_ih': _L0_gnn_in['b_ih'], 'L0_gnn_b_hh': _L0_gnn_in['b_hh']}

def reference(x, src, dst, L0_gnn_W_msg, L0_gnn_b_msg, L0_gnn_W_ih, L0_gnn_W_hh, L0_gnn_b_ih, L0_gnn_b_hh):
    import jax
    import jax.numpy as jnp

    def _L0_gnn_ref(x, edge_index, W_msg, b_msg, W_ih, W_hh, b_ih, b_hh):
        import jax, jax.numpy as jnp
        import numpy as np
        N_NODES = 3125
        N_EDGES = 18750
        H = 128
        NUM_STEPS = 5
        num_nodes = x.shape[0]
        row, col = (edge_index[0], edge_index[1])

        def step(h, _):
            messages = h[col] @ W_msg.T + b_msg
            agg = jax.ops.segment_sum(messages, row, num_segments=num_nodes)
            gi = agg @ W_ih.T + b_ih
            gh = h @ W_hh.T + b_hh
            i_r, i_z, i_n = jnp.split(gi, 3, axis=-1)
            h_r, h_z, h_n = jnp.split(gh, 3, axis=-1)
            r = jax.nn.sigmoid(i_r + h_r)
            z = jax.nn.sigmoid(i_z + h_z)
            n = jnp.tanh(i_n + r * h_n)
            h_new = (1.0 - z) * n + z * h
            return (h_new, None)
        h, _ = jax.lax.scan(step, x, None, length=NUM_STEPS)
        return h
    edge_index = jnp.stack([src, dst])
    h = jnp.maximum(_layernorm(x, axis=-1), 0.0)
    x = x + _L0_gnn_ref(h, edge_index, L0_gnn_W_msg, L0_gnn_b_msg, L0_gnn_W_ih, L0_gnn_W_hh, L0_gnn_b_ih, L0_gnn_b_hh)
    return x

_drawn_inputs = setup_inputs


def setup_inputs(seed=0):
    import zlib

    import numpy as np

    out = dict(_drawn_inputs(seed))
    spreads = {}
    factors = {}
    for name, (base, spread) in spreads.items():
        noise = np.random.default_rng([zlib.crc32(name.encode()), seed]).standard_normal(out[name].shape)
        drawn = base * np.exp(spread * noise) if base else spread * noise
        out[name] = jnp.asarray(drawn.astype(out[name].dtype))
    for name, factor in factors.items():
        out[name] = (out[name] * factor).astype(out[name].dtype)
    return out
```

```python
import concourse.bass as bass
from concourse import mybir
from contextlib import ExitStack


def gnn_gated_recurrent_kernel(nc, x, src, dst, W_msg, b_msg, W_ih, W_hh, b_ih, b_hh, out):
    f32, f16, i32 = mybir.dt.float32, mybir.dt.float16, mybir.dt.int32
    ALU, ACT, AX = mybir.AluOpType, mybir.ActivationFunctionType, mybir.AxisListType

    N, H = x.shape
    E = src.shape[0]
    STEPS = 5
    P = 128
    NCH = (N + P - 1) // P
    LASTP = N - (NCH - 1) * P
    TW = 512
    NT = (N + TW - 1) // TW
    TQ = TW // P
    RS = N + 1
    WIDTH = [min(TW, N - TW * j) for j in range(NT)]
    CHUNKS = [[(k, min(P, N - P * k)) for k in range(TQ * j, min(TQ * j + TQ, NCH))] for j in range(NT)]

    BLK = 5
    NB = N // BLK
    RH = 25
    RL = N // RH
    SW, LW = 128, RL + 1
    CAP = 256
    NS = CAP // P
    BG = 125
    NG = NB // BG
    SEG = 256
    NSMP = E // SEG
    BATCH = 5
    GRP = 25
    NGRP = NB // GRP
    BPG = GRP // BATCH
    DIV_MUL, DIV_SHIFT = 4195, 19
    assert N == NB * BLK == RH * RL and NB == NG * BG and BLK * RH == 125
    assert all((r * DIV_MUL) >> DIV_SHIFT == r // RL for r in range(N)) and N * DIV_MUL < 2 ** 24

    ET = E // 125
    UN = 3
    assert ET * 125 == E and ET % UN == 0 and STEPS % 2 == 1

    adj_dram = nc.dram_tensor("adj_scratch", [N, N], f16).ap()
    counts_dram = adj_dram.rearrange("(b c) (h l) -> (c h) b l", c=BLK, l=RL)
    msg_dram = nc.dram_tensor("msg_scratch", [N, H], f32).ap()

    with ExitStack() as ctx:
        def sb(name, shape, dt):
            return ctx.enter_context(nc.sbuf_tensor(name, shape, dt))

        def sem(name):
            return ctx.enter_context(nc.semaphore(name))

        adj = sb("adj", [P, NCH * RS], f16)
        hT = sb("hT", [P, RS], f32)
        msgs = sb("msgs", [P, 2 * NCH * 2 * H], f16)
        work = sb("work", [P, 5, TW], f32)
        aggT, rS, zS, nS, tS = (work[:, i, :] for i in range(5))
        WmT = sb("WmT", [P, H], f32)
        WihT = sb("WihT", [P, 3, H], f32)
        WhhT = sb("WhhT", [P, 3, H], f32)
        ident = sb("ident", [P, P], f32)
        iota = sb("iota", [P, P], f16)
        ones = sb("ones", [1, P], f32)
        bmrow = sb("bmrow", [1, H], f32)
        bcol = sb("bcol", [P, 8], f32)
        brz = sb("brz", [P, 2], f32)
        bnd = sb("bnd", [P, 4], f32)
        bndi = bnd[:, :].bitcast(i32)
        flag = sb("flag", [1, 1], i32)
        g_idx = sb("g_idx", [P, 1], i32)
        small = sb("small", [P, 40], f32)
        invs = bnd[:, 3:4]

        early = adj[:, :].bitcast(f32)
        take = [0]

        def carve(n, dt=f32):
            a = early[:, take[0]:take[0] + n]
            take[0] += n
            return a if dt is f32 else a.bitcast(dt)

        xs = carve(NCH * H).rearrange("p (k f) -> p k f", f=H)
        wnat = carve(7 * H).rearrange("p (k f) -> p k f", f=H)
        bnst = carve(NCH * 6).rearrange("p (k s) -> p k s", s=6)
        bnmv = carve(NCH * 2).rearrange("p (k s) -> p k s", s=2)
        lnve, lnsd, lnrs, lnnm = (carve(NCH) for _ in range(4))
        smp_i = carve(NSMP, i32)
        smp_f = carve(NSMP)
        junk = carve(SEG * 2)
        seg_i = carve(NG * SEG, i32).rearrange("p (g e) -> p g e", g=NG)
        seg_f = carve(NG * SEG).rearrange("p (g e) -> p g e", g=NG)
        dst_i = carve(NG * CAP, i32).rearrange("p (g e) -> p g e", g=NG)
        src_i = carve(NG * CAP, i32).rearrange("p (g e) -> p g e", g=NG)
        cl_f = carve(NG * CAP).rearrange("p (g e) -> p g e", g=NG)
        rm_i = carve(NG * CAP, i32).rearrange("p (g e) -> p g e", g=NG)
        rh_i = carve(NG * CAP, i32).rearrange("p (g e) -> p g e", g=NG)
        sk_f = carve(NG * CAP).rearrange("p (g e) -> p g e", g=NG)
        sc_f = carve(NG * CAP).rearrange("p (g e) -> p g e", g=NG)
        lk_f = carve(NG * CAP).rearrange("p (g e) -> p g e", g=NG)
        blk_i = carve(NG, i32)
        off_i = carve(NG, i32)
        start_i = carve(NG, i32)
        blk_f, cnt_a, off_f, cnt_b, start_f = (small[:, 5 * i:5 * i + 5] for i in range(5))
        nlow, nhigh, nval, onecol, tot = (small[:, 25 + i:26 + i] for i in range(5))
        assert take[0] < (NCH - 1) * RS // 2

        keys = work[:, :, :].rearrange("p a b -> p (a b)").bitcast(f16)
        skey = keys[:, 0:NB * NS * 2]
        lkey = keys[:, NB * NS * 2:2 * NB * NS * 2]
        OHN = BATCH * NS
        oh_mem = [msgs[:, 2 * GRP * RL:], msgs[:, 2 * GRP * RL + OHN * (SW + LW):], adj[:, (NCH - 1) * RS:]]
        ohS = [m[:, 0:OHN * SW].rearrange("p (t j) -> p t j", t=OHN) for m in oh_mem]
        ohL = [m[:, OHN * SW:OHN * (SW + LW)].rearrange("p (t j) -> p t j", t=OHN) for m in oh_mem]
        stage = msgs[:, 0:2 * GRP * RL]

        g_iota = early[:, 0:N]
        g_one = early[:, N:2 * N]
        g_dst = early[:, 2 * N:2 * N + ET].bitcast(i32)
        g_srci = early[:, 2 * N + ET:2 * N + 2 * ET].bitcast(i32)
        g_src = early[:, 2 * N + 2 * ET:2 * N + 3 * ET]
        g_msg = early[:, 7 * ET + 2 * N:7 * ET + 2 * N + H]
        g_agg = early[:, 8 * ET + 2 * N:8 * ET + 3 * N]
        g_node = early[:, 8 * ET + 3 * N:8 * ET + 3 * N + NCH * H]

        ps = ctx.enter_context(nc.psum_tensor("ps", [P, 8, TW], f32))
        pflat = ps[:, :, :].rearrange("p b n -> p (b n)")
        psAgg = [ps[:, 0, :], ps[:, 1, :]]
        psR, psZ, psI, psH, psM = (ps[:, i, :] for i in range(2, 7))
        psX = ps[:, 7, :]
        blkps = [pflat[:, 2 * TW * i:2 * TW * (i + 1)].rearrange("p (b j) -> p b j", j=P) for i in range(3)]

        consts = sem("consts")
        x_padded = sem("x_padded")
        x_loaded = sem("x_loaded")
        w_loaded = sem("w_loaded")
        b_loaded = sem("b_loaded")
        smp_loaded = sem("smp_loaded")
        smp_conv = sem("smp_conv")
        smp_spread = sem("smp_spread")
        coarse_off = sem("coarse_off")
        seg_loaded = sem("seg_loaded")
        fine_off = sem("fine_off")
        win_loaded = sem("win_loaded")
        dv = sem("dv")
        ln_var = sem("ln_var")
        ln_sd = sem("ln_sd")
        ln_scale = sem("ln_scale")
        x_normed = sem("x_normed")
        xT_ready = sem("xT_ready")
        h0_ready = sem("h0_ready")
        wT_ready = sem("wT_ready")
        wT_copied = sem("wT_copied")
        wm_scaled = sem("wm_scaled")
        bm_ready = sem("bm_ready")
        keys_ready = sem("keys_ready")
        keyT_ready = sem("keyT_ready")
        keyT_copied = sem("keyT_copied")
        nval_ready = sem("nval_ready")
        nval_summed = sem("nval_summed")
        flag_ready = sem("flag_ready")
        onehots_ready = sem("onehots_ready")
        blocks_done = sem("blocks_done")
        counts_staged = sem("counts_staged")
        stage_written = sem("stage_written")
        adj_loaded = sem("adj_loaded")
        last_cleared = sem("last_cleared")
        agg_done = sem("agg_done")
        aggT_ready = sem("aggT_ready")
        r_summed = sem("r_summed")
        z_summed = sem("z_summed")
        n_summed = sem("n_summed")
        r_ready = sem("r_ready")
        z_ready = sem("z_ready")
        gated = sem("gated")
        n_arg = sem("n_arg")
        n_ready = sem("n_ready")
        h_minus_n = sem("h_minus_n")
        z_times = sem("z_times")
        h_ready = sem("h_ready")
        msg_done = sem("msg_done")
        msg_hi = sem("msg_hi")
        msg_lo = sem("msg_lo")
        x_again = sem("x_again")
        outT_done = sem("outT_done")
        out_added = sem("out_added")
        out_written = sem("out_written")
        g_consts = sem("g_consts")
        g_edges = sem("g_edges")
        g_conv = sem("g_conv")
        g_index = sem("g_index")
        g_node_ready = sem("g_node_ready")
        g_node_sum = sem("g_node_sum")
        g_node_written = sem("g_node_written")
        g_gathered = [sem(f"g_gathered{i}") for i in range(UN)]
        g_onehot = sem("g_onehot")
        g_tile_done = sem("g_tile_done")
        g_copied = sem("g_copied")
        pool_turn = sem("pool_turn")
        sp_turn = sem("sp_turn")
        block = ctx.enter_context(nc.Block())

        def past(n):
            return n + 1

        def mpart(par, k, part):
            return par * (NCH * 2 * H) + (k * 2 + part) * H

        @block.sync
        def _(sp):
            ctx.enter_context(nc.allow_non_contiguous_dma(reason="samples and bias columns: a few hundred single elements"))
            sp.dma_start(smp_i[0:1, :], dst[0:NSMP * SEG].rearrange("(a n s) -> a n s", a=1, s=SEG)[:, :, SEG - 1]
                         ).then_inc(smp_loaded, 16)
            sp.dma_start(xs[:, 0:NCH - 1, :], x[0:(NCH - 1) * P, :].rearrange("(k p) f -> p k f", p=P)
                         ).then_inc(x_loaded, 16)
            sp.wait_ge(x_padded, 1)
            sp.dma_start(xs[0:LASTP, NCH - 1, :], x[(NCH - 1) * P:N, :]).then_inc(x_loaded, 16)
            sp.dma_start(wnat[:, 0, :], W_msg).then_inc(w_loaded, 16)
            sp.dma_start(wnat[:, 1:4, :], W_ih.rearrange("(g p) f -> p g f", p=P)).then_inc(w_loaded, 16)
            sp.dma_start(wnat[:, 4:7, :], W_hh.rearrange("(g p) f -> p g f", p=P)).then_inc(w_loaded, 16)
            sp.dma_start(bcol[:, 0:3], b_ih.rearrange("(g p) -> p g", p=P)).then_inc(b_loaded, 16)
            sp.dma_start(bcol[:, 3:6], b_hh.rearrange("(g p) -> p g", p=P)).then_inc(b_loaded, 16)
            sp.dma_start(bcol[:, 6:7], b_msg.rearrange("(p a) -> p a", a=1)).then_inc(b_loaded, 16)
            sp.wait_ge(flag_ready, 1)
            fast = sp.value_load(flag[0:1, 0:1], min_val=0, max_val=1)
            with sp.If(fast):
                def write_counts(g, first):
                    sp.wait_ge(counts_staged, BPG * (g + 1))
                    sp.sem_inc(sp_turn, 1)
                    if not first:
                        sp.wait_ge(stage_written, 32 * g)
                        sp.sem_inc(sp_turn, 1)
                    slot = stage[:, bass.ds((g % 2) * (GRP * RL), GRP * RL)].rearrange("p (b j) -> p b j", j=RL)
                    to = counts_dram[:, bass.ds(g * GRP, GRP), :]
                    sp.dma_start(to[0:120], slot[0:120]).then_inc(stage_written, 16)
                    sp.dma_start(to[120:125], slot[120:125]).then_inc(stage_written, 16)

                write_counts(0, True)
                with sp.Fori(1, NGRP) as g:
                    write_counts(g, False)
                sp.wait_ge(agg_done, past(NT * (STEPS - 1)))
                xres = msgs[:, mpart(1, 0, 0):].bitcast(f32).rearrange("p (k f) -> p k f", f=H)
                sp.dma_start(xres[:, 0:NCH - 1, :], x[0:(NCH - 1) * P, :].rearrange("(k p) f -> p k f", p=P)
                             ).then_inc(x_again, 16)
                sp.dma_start(xres[0:LASTP, NCH - 1, :], x[(NCH - 1) * P:N, :]).then_inc(x_again, 16)
                for j in range(NT):
                    sp.wait_ge(out_added, j + 1)
                    k0, n = CHUNKS[j][0][0], len(CHUNKS[j])
                    if WIDTH[j] == TW:
                        sp.dma_start(out[TW * j:TW * (j + 1), :].rearrange("(k p) f -> p k f", p=P),
                                     xres[:, k0:k0 + n, :]).then_inc(out_written, 16)
                    else:
                        sp.dma_start(out[TW * j:N, :], xres[0:LASTP, k0, :]).then_inc(out_written, 16)
                sp.wait_ge(out_written, 16 * NT)
            with sp.Else():
                sp.dma_start(g_dst[0:125, :], dst.rearrange("(p t) -> p t", t=ET)).then_inc(g_edges, 16)
                sp.dma_start(g_srci[0:125, :], src.rearrange("(p t) -> p t", t=ET)).then_inc(g_edges, 16)
                node = g_node.rearrange("p (k f) -> p k f", f=H)
                with sp.Fori(0, STEPS) as s:
                    sp.wait_ge(g_node_ready, past(NT * (s + 1)))
                    sp.sem_inc(sp_turn, 1)
                    sp.dma_start(msg_dram[0:(NCH - 1) * P, :].rearrange("(k p) f -> p k f", p=P),
                                 node[:, 0:NCH - 1, :]).then_inc(g_node_written, 16)
                    sp.dma_start(msg_dram[(NCH - 1) * P:N, :], node[0:LASTP, NCH - 1, :]).then_inc(g_node_written, 16)
                sp.wait_ge(agg_done, past(STEPS * NT))
                sp.wait_ge(h_ready, past(STEPS * NT))
                sp.dma_start(node[:, 0:NCH - 1, :], x[0:(NCH - 1) * P, :].rearrange("(k p) f -> p k f", p=P)
                             ).then_inc(x_again, 16)
                sp.dma_start(node[0:LASTP, NCH - 1, :], x[(NCH - 1) * P:N, :]).then_inc(x_again, 16)
                sp.wait_ge(out_added, NT)
                sp.dma_start(out[0:(NCH - 1) * P, :].rearrange("(k p) f -> p k f", p=P),
                             node[:, 0:NCH - 1, :]).then_inc(out_written, 16)
                sp.dma_start(out[(NCH - 1) * P:N, :], node[0:LASTP, NCH - 1, :]).then_inc(out_written, 16)
                sp.wait_ge(out_written, 32)

        @block.gpsimd
        def _(pool):
            pool.iota(blk_i[0:BG, :], pattern=[[BLK * BG, NG]], base=0, channel_multiplier=BLK).then_inc(consts, 1)
            pool.memset(ident[:, :], 0.0).then_inc(consts, 1)
            pool.memset(ones[:, :], 1.0).then_inc(consts, 1)
            pool.wait_ge(consts, 3)
            pool.affine_select(out=ident[:, :], in_=ident[:, :], compare_op=ALU.not_equal, fill=1.0, base=0,
                               pattern=[[-1, P]], channel_multiplier=1).then_inc(consts, 1)
            pool.iota(iota[:, :], pattern=[[1, P]], base=0, channel_multiplier=0,
                      allow_small_or_imprecise_dtypes=True).then_inc(consts, 1)
            flat = [a.rearrange("(a b) -> a b", a=1) for a in (dst, src)]

            def gather(to, g, offsets, of, done):
                pool.indirect_dma_start(out=to[0:BG, g, :], out_offset=None, in_=flat[of],
                                        in_offset=bass.IndirectOffsetOnAxis(ap=offsets[0:BG, g:g + 1], axis=1)
                                        ).then_inc(done, 16)

            pool.wait_ge(coarse_off, 1)
            for g in range(NG):
                gather(seg_i, g, off_i, 0, seg_loaded)
            pool.wait_ge(fine_off, 1)
            for g in range(NG):
                gather(dst_i, g, start_i, 0, win_loaded)
                gather(src_i, g, start_i, 1, win_loaded)
            pool.wait_ge(flag_ready, 1)
            fast = pool.value_load(flag[0:1, 0:1], min_val=0, max_val=1)
            with pool.If(fast):
                def load_chunk(k, groups, rows, first=False):
                    pool.wait_ge(stage_written, 32 * groups)
                    if not first:
                        pool.wait_ge(adj_loaded, 16 * k)
                    pool.dma_start(adj[0:rows, bass.ds(k * RS, N)], adj_dram[bass.ds(k * P, rows), :]
                                   ).then_inc(adj_loaded, 16)

                pool.wait_ge(keyT_copied, 2 * NG)
                pool.wait_ge(h0_ready, NT)
                load_chunk(0, 2, P, first=True)
                with pool.Fori(1, NCH - 2) as k:
                    load_chunk(k, k + 2, P)
                load_chunk(NCH - 2, NGRP, P)
                pool.wait_ge(last_cleared, 1)
                load_chunk(NCH - 1, NGRP, LASTP)
            with pool.Else():
                pool.wait_ge(keyT_copied, 2 * NG)
                pool.wait_ge(h0_ready, NT)
                pool.iota(g_iota, pattern=[[1, N]], base=0, channel_multiplier=0,
                          allow_small_or_imprecise_dtypes=True).then_inc(g_consts, 1)
                pool.wait_ge(g_edges, 32)
                with pool.Fori(0, STEPS) as s:
                    pool.wait_ge(g_node_written, 32 * (s + 1))
                    pool.sem_inc(pool_turn, 1)
                    with pool.Fori(0, ET // UN) as u:
                        for i in range(UN):
                            pool.wait_ge(g_index, s * ET + u * UN + (i + 1))
                            pool.sem_inc(pool_turn, 1)
                            pool.indirect_dma_start(
                                out=g_msg[0:125, :], out_offset=None, in_=msg_dram,
                                in_offset=bass.IndirectOffsetOnAxis(ap=g_idx[0:125, :], axis=0)
                            ).then_inc(g_gathered[i], 16)

        @block.vector
        def _(v):
            for started in (n_arg, h_ready, g_node_ready):
                v.sem_inc(started, 1)
            chain = [0]

            def link(ins):
                chain[0] += 1
                ins.then_inc(dv, 1)
                v.wait_ge(dv, chain[0])

            nc.vector.memset(xs[0:P, NCH - 1, :], 0.0).then_inc(x_padded, 1)
            link(nc.vector.memset(small[:, :], 0.0))
            link(nc.vector.memset(onecol[:, :], 1.0))
            v.wait_ge(smp_loaded, 16)
            nc.vector.tensor_copy(smp_f[0:1, :], smp_i[0:1, :]).then_inc(smp_conv, 1)
            v.wait_ge(consts, 5)
            link(nc.vector.tensor_copy(blk_f[0:BG, :], blk_i[0:BG, :]))
            v.wait_ge(smp_spread, 1)
            for g in range(NG):
                link(nc.vector.tensor_scalar(junk[0:BG, 0:NSMP], psX[0:BG, 0:NSMP], blk_f[0:BG, g:g + 1], None,
                                             ALU.is_lt, op1=ALU.add, accum_out=cnt_a[0:BG, g:g + 1]))
            link(nc.vector.tensor_scalar(off_f[0:BG, :], cnt_a[0:BG, :], float(SEG), float(E - SEG), ALU.mult, ALU.min))
            nc.vector.tensor_copy(off_i[0:BG, :], off_f[0:BG, :]).then_inc(coarse_off, 1)
            v.wait_ge(x_loaded, 32)
            for k in range(NCH):
                nc.vector.bn_stats(bnst[:, k, :], xs[:, k, :]).then_inc(dv, 1)
            chain[0] += NCH
            v.wait_ge(dv, chain[0])
            for k in range(NCH):
                nc.vector.bn_aggr(bnmv[:, k, :], bnst[:, k, :]).then_inc(dv, 1)
            chain[0] += NCH
            v.wait_ge(dv, chain[0])
            nc.vector.tensor_scalar(lnve, bnmv[:, :, 1], 1e-5, None, ALU.add).then_inc(ln_var, 1)
            v.wait_ge(seg_loaded, 16 * NG)
            link(nc.vector.tensor_copy(seg_f[0:BG], seg_i[0:BG]))
            for g in range(NG):
                link(nc.vector.tensor_scalar(junk[0:BG, 0:SEG], seg_f[0:BG, g, :], blk_f[0:BG, g:g + 1], None,
                                             ALU.is_lt, op1=ALU.add, accum_out=cnt_b[0:BG, g:g + 1]))
            link(nc.vector.tensor_tensor(start_f[0:BG, :], off_f[0:BG, :], cnt_b[0:BG, :], ALU.add))
            nc.vector.tensor_scalar(start_i[0:BG, :], start_f[0:BG, :], float(E - CAP), None, ALU.min
                                    ).then_inc(fine_off, 1)
            v.wait_ge(ln_sd, 1)
            link(nc.vector.reciprocal(lnrs, lnsd))
            nc.vector.scalar_tensor_tensor(out=lnnm, in0=bnmv[:, :, 0], scalar=-1.0, in1=lnrs,
                                           op0=ALU.mult, op1=ALU.mult).then_inc(ln_scale, 1)
            v.wait_ge(w_loaded, 48)
            v.wait_ge(b_loaded, 48)
            link(nc.vector.tensor_reduce(bnd[:, 0:1], wnat[:, 0, :], AX.X, ALU.add, apply_absolute_value=True))
            link(nc.vector.tensor_scalar(bcol[:, 7:8].bitcast(i32), bcol[:, 6:7].bitcast(i32), 0x7FFFFFFF, None,
                                         ALU.bitwise_and))
            link(nc.vector.tensor_scalar(bnd[:, 1:2], bnd[:, 0:1], 12.0, 1e-30, ALU.mult, ALU.add))
            link(nc.vector.tensor_tensor(bnd[:, 0:1], bnd[:, 1:2], bcol[:, 7:8], ALU.add))
            link(nc.vector.tensor_scalar(bndi[:, 1:2], bndi[:, 0:1], 0x7F800000, None, ALU.bitwise_and))
            link(nc.vector.tensor_scalar(bndi[:, 2:3], bndi[:, 1:2], 0x7F800000, None, ALU.bitwise_xor))
            link(nc.vector.tensor_scalar(bnd[:, 2:3], bnd[:, 2:3], float(2 ** 13), None, ALU.mult))
            link(nc.vector.tensor_scalar(bnd[:, 3:4], bnd[:, 1:2], float(2 ** -14), None, ALU.mult))
            link(nc.vector.tensor_tensor(brz[:, :], bcol[:, 0:2], bcol[:, 3:5], ALU.add))
            link(nc.vector.tensor_scalar(bcol[:, 7:8], bcol[:, 6:7], bnd[:, 2:3], None, ALU.mult))
            nc.vector.tensor_scalar(wnat[:, 0, :], wnat[:, 0, :], bnd[:, 2:3], None, ALU.mult).then_inc(wm_scaled, 1)
            v.wait_ge(win_loaded, 32 * NG)
            link(nc.vector.tensor_tensor(cl_f[0:BG], dst_i[0:BG],
                                         blk_f[0:BG, :].rearrange("p (g o) -> p g o", o=1).broadcast_to([BG, NG, CAP]),
                                         ALU.subtract))
            link(nc.vector.tensor_scalar(rm_i[0:BG], src_i[0:BG], float(DIV_MUL), None, ALU.mult))
            link(nc.vector.tensor_scalar(rh_i[0:BG], rm_i[0:BG], DIV_SHIFT, None, ALU.logical_shift_right))
            link(nc.vector.scalar_tensor_tensor(out=sk_f[0:BG], in0=cl_f[0:BG], scalar=float(RH), in1=rh_i[0:BG],
                                                op0=ALU.mult, op1=ALU.add))
            link(nc.vector.tensor_scalar(sc_f[0:BG], sk_f[0:BG], -1.0, 255.0, ALU.max, ALU.min))
            nc.vector.scalar_tensor_tensor(out=lk_f[0:BG], in0=rh_i[0:BG], scalar=float(-RL), in1=src_i[0:BG],
                                           op0=ALU.mult, op1=ALU.add).then_inc(keys_ready, 1)
            link(nc.vector.tensor_scalar(seg_f[0:BG], cl_f[0:BG], float(BLK), None, ALU.is_lt, op1=ALU.add,
                                         accum_out=nlow[0:BG, :]))
            link(nc.vector.tensor_scalar(seg_f[0:BG], cl_f[0:BG], 0.0, None, ALU.is_lt, op1=ALU.add,
                                         accum_out=nhigh[0:BG, :]))
            nc.vector.tensor_tensor(nval[:, :], nlow[:, :], nhigh[:, :], ALU.subtract).then_inc(nval_ready, 1)
            v.wait_ge(wT_ready, 1)
            nc.vector.tensor_copy(WmT[:, :], ps[:, 0, 0:P]).then_inc(wT_copied, 1)
            nc.vector.tensor_copy(WihT[:, :, :], ps[:, 0, P:4 * P].rearrange("p (g f) -> p g f", g=3)).then_inc(wT_copied, 1)
            nc.vector.tensor_copy(WhhT[:, :, :], ps[:, 1, 0:3 * P].rearrange("p (g f) -> p g f", g=3)).then_inc(wT_copied, 1)
            nc.vector.tensor_copy(bmrow[:, :], ps[0:1, 1, 3 * P:4 * P]).then_inc(wT_copied, 1)
            for j in range(NT):
                v.wait_ge(xT_ready, j + 1)
                nc.vector.tensor_copy(hT[:, TW * j:TW * j + WIDTH[j]], ps[:, 2 + j % 2, 0:WIDTH[j]]).then_inc(h0_ready, 1)
            for i in range(2 * NG):
                g, key = i // 2, (skey, lkey)[i % 2]
                v.wait_ge(keyT_ready, i + 1)
                nc.vector.tensor_copy(
                    key.rearrange("p (b s d) -> p b s d", s=NS, d=2)[:, BG * g:BG * (g + 1)],
                    ps[:, 4 + i % 2, 0:NS * P].rearrange("p (s b d) -> p b s d", s=NS, d=1)[:, 0:BG]
                    .broadcast_to([P, BG, NS, 2])).then_inc(keyT_copied, 1)
            v.wait_ge(nval_summed, 1)
            nc.vector.tensor_scalar(flag[0:1, 0:1], psX[0:1, 0:1], float(E), None, ALU.is_equal).then_inc(flag_ready, 1)
            v.wait_ge(flag_ready, 1)
            fast = v.value_load(flag[0:1, 0:1], min_val=0, max_val=1)

            def gates(g, cols, w, hread=True):
                v.wait_ge(r_ready, past(g + 1))
                v.wait_ge(n_summed, g + 1)
                v.wait_ge(n_ready, past(g))
                nc.vector.scalar_tensor_tensor(out=tS[:, 0:w], in0=psH[:, 0:w], scalar=bcol[:, 5:6], in1=rS[:, 0:w],
                                               op0=ALU.add, op1=ALU.mult).then_inc(gated, 1)
                v.wait_ge(gated, g + 1)
                nc.vector.tensor_tensor(tS[:, 0:w], psI[:, 0:w], tS[:, 0:w], ALU.add).then_inc(n_arg, 1)
                v.wait_ge(n_ready, past(g + 1))
                h = hT[:, cols:cols + w]
                nc.vector.tensor_tensor(rS[:, 0:w], h, nS[:, 0:w], ALU.subtract).then_inc(h_minus_n, 1)
                v.wait_ge(h_minus_n, g + 1)
                v.wait_ge(z_ready, past(g + 1))
                nc.vector.tensor_tensor(rS[:, 0:w], rS[:, 0:w], zS[:, 0:w], ALU.mult).then_inc(z_times, 1)
                v.wait_ge(z_times, g + 1)
                nc.vector.tensor_tensor(h, rS[:, 0:w], nS[:, 0:w], ALU.add).then_inc(h_ready, 1)

            def lo_part(m, par, j):
                v.wait_ge(msg_hi, m + 1)
                rows, n, k0 = CHUNKS[j][-1][1], len(CHUNKS[j]), CHUNKS[j][0][0]
                tile = msgs[0:rows, mpart(par, k0, 0):mpart(par, k0 + n, 0)].rearrange("p (k a f) -> p k a f", a=2, f=H)
                nc.vector.tensor_tensor(tile[:, :, 1, :], psM[0:rows, 0:n * H].rearrange("p (k f) -> p k f", f=H),
                                        tile[:, :, 0, :], ALU.subtract).then_inc(msg_lo, 1)

            with v.If(fast):
                def onehots(q, b, kcol, prior):
                    if prior is not None:
                        v.wait_ge(blocks_done, prior)
                    for oh, key, w in ((ohS, skey, SW), (ohL, lkey, LW)):
                        k4 = key[:, bass.ds(kcol, OHN * 2)].rearrange("p (t o d) -> p t o d", o=1, d=2)
                        i4 = iota[:, 0:w].rearrange("p (o j d) -> p o j d", o=1, d=2)
                        shape = [P, OHN, w // 2, 2]
                        nc.vector.tensor_tensor(oh[b % 3].rearrange("p t (j d) -> p t j d", d=2),
                                                k4.broadcast_to(shape), i4.broadcast_to(shape), ALU.is_equal
                                                ).then_inc(onehots_ready, 1)

                PRIOR = [2, 2, 5, 3, 3]
                for b in range(BPG):
                    onehots(b, b, b * OHN * 2, b - 2 if b >= 3 else None)
                with v.Fori(1, NGRP) as g:
                    for b in range(BPG):
                        onehots(None, b, g * (GRP * NS * 2) + b * OHN * 2, g * BPG + (b - PRIOR[b] + 1))
                v.wait_ge(blocks_done, NGRP * BPG)
                nc.vector.memset(adj[0:P, (NCH - 1) * RS:NCH * RS], 0.0).then_inc(last_cleared, 1)
                v.wait_ge(stage_written, 32 * NGRP)
                link(nc.vector.memset(msgs[0:P, mpart(0, NCH - 1, 0):mpart(0, NCH - 1, 2)], 0.0))
                link(nc.vector.memset(msgs[0:P, mpart(1, NCH - 1, 0):mpart(1, NCH - 1, 2)], 0.0))

                for j in range(NT - 2):
                    lo_part(j, 0, j)

                def step(s, par, last):
                    nxt, g0 = 1 - par, s * NT
                    lo_part(g0 + NT - 2, par, NT - 2)
                    lo_part(g0 + NT - 1, par, NT - 1)
                    for j in range(NT):
                        gates(g0 + j, TW * j, WIDTH[j])
                        if not last and 1 <= j < NT - 1:
                            lo_part(g0 + NT + j - 1, nxt, j - 1)
                        if last and j >= 1:
                            add_x(j - 1)
                    if last:
                        add_x(NT - 1)

                xres = msgs[:, mpart(1, 0, 0):].bitcast(f32).rearrange("p (k f) -> p k f", f=H)

                def add_x(j):
                    v.wait_ge(outT_done, j + 1)
                    if j == 0:
                        v.wait_ge(x_again, 32)
                    rows, n, k0 = CHUNKS[j][-1][1], len(CHUNKS[j]), CHUNKS[j][0][0]
                    nc.vector.tensor_tensor(xres[0:rows, k0:k0 + n, :],
                                            psM[0:rows, 0:n * H].rearrange("p (k f) -> p k f", f=H),
                                            xres[0:rows, k0:k0 + n, :], ALU.add).then_inc(out_added, 1)

                with v.Fori(0, STEPS - 1, 2) as s:
                    step(s, 0, False)
                    step(s + 1, 1, False)
                step(STEPS - 1, 0, True)
            with v.Else():
                v.wait_ge(g_edges, 32)
                nc.vector.tensor_copy(g_src[0:125, :], g_srci[0:125, :]).then_inc(g_conv, 1)
                v.wait_ge(g_conv, 1)
                v.wait_ge(g_consts, 1)
                node = g_node.rearrange("p (k f) -> p k f", f=H)
                with v.Fori(0, STEPS) as s:
                    for j in range(NT):
                        rows, n, k0 = CHUNKS[j][-1][1], len(CHUNKS[j]), CHUNKS[j][0][0]
                        v.wait_ge(g_node_sum, s * NT + j + 1)
                        v.wait_ge(agg_done, past(NT * s))
                        nc.vector.tensor_copy(node[0:rows, k0:k0 + n, :],
                                              psM[0:rows, 0:n * H].rearrange("p (k f) -> p k f", f=H)
                                              ).then_inc(g_node_ready, 1)
                    with v.Fori(0, ET) as t:
                        v.wait_ge(g_tile_done, past(s * ET + t))
                        nc.vector.tensor_copy(g_idx[0:125, :], g_dst[0:125, bass.ds(t, 1)]).then_inc(g_index, 1)
                        nc.vector.tensor_scalar(g_one[0:125, :], g_iota[0:125, :], g_src[0:125, bass.ds(t, 1)], None,
                                                ALU.is_equal).then_inc(g_onehot, 1)
                    v.wait_ge(agg_done, past(NT * (s + 1)))
                    for j in range(NT):
                        nc.vector.tensor_scalar(g_agg[:, TW * j:TW * j + WIDTH[j]], ps[:, j, 0:WIDTH[j]], invs, None,
                                                ALU.mult).then_inc(g_copied, 1)
                    for j in range(NT):
                        gates(s * NT + j, TW * j, WIDTH[j])
                v.wait_ge(x_again, 32)
                for j in range(NT):
                    rows, n, k0 = CHUNKS[j][-1][1], len(CHUNKS[j]), CHUNKS[j][0][0]
                    v.wait_ge(outT_done, j + 1)
                    nc.vector.tensor_tensor(node[0:rows, k0:k0 + n, :],
                                            psM[0:rows, 0:n * H].rearrange("p (k f) -> p k f", f=H),
                                            node[0:rows, k0:k0 + n, :], ALU.add).then_inc(out_added, 1)

        @block.scalar
        def _(act):
            for started in (r_ready, z_ready, n_ready, aggT_ready):
                act.sem_inc(started, 1)
            act.wait_ge(ln_var, 1)
            nc.scalar.activation(lnsd, lnve, ACT.Sqrt).then_inc(ln_sd, 1)
            act.wait_ge(ln_scale, 1)
            for k in range(NCH):
                nc.scalar.activation(xs[:, k, :], xs[:, k, :], ACT.Relu, bias=lnnm[:, k:k + 1],
                                     scale=lnrs[:, k:k + 1]).then_inc(x_normed, 1)
            act.wait_ge(flag_ready, 1)
            fast = act.value_load(flag[0:1, 0:1], min_val=0, max_val=1)

            def gates(g, w):
                act.wait_ge(r_summed, g + 1)
                act.wait_ge(h_ready, past(g))
                nc.scalar.activation(rS[:, 0:w], psR[:, 0:w], ACT.Sigmoid, bias=brz[:, 0:1]).then_inc(r_ready, 1)
                act.wait_ge(z_summed, past(g + 1))
                nc.scalar.activation(zS[:, 0:w], psZ[:, 0:w], ACT.Sigmoid, bias=brz[:, 1:2]).then_inc(z_ready, 1)
                act.wait_ge(n_arg, past(g + 1))
                nc.scalar.activation(nS[:, 0:w], tS[:, 0:w], ACT.Tanh, bias=bcol[:, 2:3]).then_inc(n_ready, 1)

            with act.If(fast):
                def stage_batch(b, col, ready, free):
                    act.wait_ge(blocks_done, ready)
                    if free is not None:
                        act.wait_ge(stage_written, free)
                    nc.scalar.activation(stage[0:125, bass.ds(col, BATCH * RL)].rearrange("p (b j) -> p b j", j=RL),
                                         blkps[b % 3][0:125, 0:BATCH, 0:RL], ACT.Copy).then_inc(counts_staged, 1)

                for g in range(2):
                    for b in range(BPG):
                        stage_batch(b, (g * GRP + b * BATCH) * RL, g * BPG + b + 1, None)
                with act.Fori(2, NGRP) as g:
                    for b in range(BPG):
                        stage_batch(b, (g % 2) * (GRP * RL) + b * BATCH * RL, g * BPG + b + 1,
                                    32 * (g - 1) if b == 0 else None)

                def evac(g, j):
                    act.wait_ge(agg_done, past(g + 1))
                    act.wait_ge(z_summed, past(g))
                    nc.scalar.activation(aggT[:, 0:WIDTH[j]], psAgg[j % 2][:, 0:WIDTH[j]], ACT.Identity, scale=invs
                                         ).then_inc(aggT_ready, 1)

                def hi_part(m, par, j):
                    act.wait_ge(msg_done, m + 1)
                    rows, n, k0 = CHUNKS[j][-1][1], len(CHUNKS[j]), CHUNKS[j][0][0]
                    tile = msgs[0:rows, mpart(par, k0, 0):mpart(par, k0 + n, 0)].rearrange("p (k a f) -> p k a f", a=2, f=H)
                    nc.scalar.activation(tile[:, :, 0, :], psM[0:rows, 0:n * H].rearrange("p (k f) -> p k f", f=H),
                                         ACT.Copy).then_inc(msg_hi, 1)

                act.wait_ge(stage_written, 32 * NGRP)
                for j in range(NT - 2):
                    hi_part(j, 0, j)

                def step(s, par, last):
                    nxt, g0 = 1 - par, s * NT
                    hi_part(g0 + NT - 2, par, NT - 2)
                    hi_part(g0 + NT - 1, par, NT - 1)
                    evac(g0, 0)
                    for j in range(NT):
                        if j < NT - 1:
                            evac(g0 + j + 1, j + 1)
                        gates(g0 + j, WIDTH[j])
                        if not last and 1 <= j < NT - 1:
                            hi_part(g0 + NT + j - 1, nxt, j - 1)

                with act.Fori(0, STEPS - 1, 2) as s:
                    step(s, 0, False)
                    step(s + 1, 1, False)
                step(STEPS - 1, 0, True)
            with act.Else():
                with act.Fori(0, STEPS) as s:
                    for j in range(NT):
                        gates(s * NT + j, WIDTH[j])

        @block.tensor
        def _(pe):
            for started in (z_summed, agg_done, g_tile_done):
                pe.sem_inc(started, 1)
            pe.wait_ge(smp_conv, 1)
            pe.wait_ge(consts, 5)
            nc.tensor.matmul(psX[0:BG, 0:NSMP], ones[0:1, 0:BG], smp_f[0:1, :], start=True, stop=True
                             ).then_inc(smp_spread, 1)
            pe.wait_ge(wm_scaled, 1)
            for i in range(7):
                nc.tensor.transpose(ps[:, i // 4, (i % 4) * P:(i % 4 + 1) * P], wnat[:, i, :], ident[:, :])
            nc.tensor.matmul(ps[0:1, 1, 3 * P:4 * P], bcol[:, 7:8], ident[:, :], start=True, stop=True
                             ).then_inc(wT_ready, 1)
            for j in range(NT):
                pe.wait_ge(x_normed, CHUNKS[j][-1][0] + 1)
                if j >= 2:
                    pe.wait_ge(h0_ready, j - 1)
                for k, rows in CHUNKS[j]:
                    last = nc.tensor.transpose(ps[:, 2 + j % 2, (k % TQ) * P:(k % TQ) * P + rows], xs[0:rows, k, :],
                                               ident[0:rows, 0:rows])
                last.then_inc(xT_ready, 1)
            pe.wait_ge(keys_ready, 1)
            for i in range(2 * NG):
                g, key = i // 2, (sc_f, lk_f)[i % 2]
                if i >= 2:
                    pe.wait_ge(keyT_copied, i - 1)
                for s in range(NS):
                    last = nc.tensor.transpose(ps[:, 4 + i % 2, s * P:s * P + BG], key[0:BG, g, s * P:(s + 1) * P],
                                               ident[0:BG, 0:BG])
                last.then_inc(keyT_ready, 1)
            pe.wait_ge(nval_ready, 1)
            nc.tensor.matmul(psX[0:1, 0:1], nval[0:BG, :], onecol[0:BG, :], start=True, stop=True
                             ).then_inc(nval_summed, 1)
            pe.wait_ge(wT_copied, 4)
            pe.wait_ge(h0_ready, NT)
            pe.wait_ge(keyT_copied, 2 * NG)
            pe.wait_ge(flag_ready, 1)
            fast = pe.value_load(flag[0:1, 0:1], min_val=0, max_val=1)

            def node_product(j):
                for k, rows in CHUNKS[j]:
                    to = psM[0:rows, (k % TQ) * H:(k % TQ + 1) * H]
                    nc.tensor.matmul(to, hT[:, P * k:P * k + rows], WmT[:, :], start=True, stop=False)
                    last = nc.tensor.matmul(to, ones[0:1, 0:rows], bmrow[0:1, :], start=False, stop=True)
                return last

            def gru_products(g, j, src_agg):
                w = WIDTH[j]
                h = hT[:, TW * j:TW * j + w]
                pe.wait_ge(r_ready, past(g))
                nc.tensor.matmul(psR[:, 0:w], WhhT[:, 0, :], h, start=True, stop=False)
                nc.tensor.matmul(psR[:, 0:w], WihT[:, 0, :], src_agg, start=False, stop=True).then_inc(r_summed, 1)
                pe.wait_ge(n_arg, past(g))
                nc.tensor.matmul(psH[:, 0:w], WhhT[:, 2, :], h, start=True, stop=True)
                nc.tensor.matmul(psI[:, 0:w], WihT[:, 2, :], src_agg, start=True, stop=True).then_inc(n_summed, 1)
                pe.wait_ge(z_ready, past(g))
                nc.tensor.matmul(psZ[:, 0:w], WhhT[:, 1, :], h, start=True, stop=False)
                nc.tensor.matmul(psZ[:, 0:w], WihT[:, 1, :], src_agg, start=False, stop=True).then_inc(z_summed, 1)

            def out_transpose(j):
                for k, rows in CHUNKS[j]:
                    last = nc.tensor.transpose(psM[0:rows, (k % TQ) * H:(k % TQ + 1) * H], hT[:, P * k:P * k + rows],
                                               ident[:, :])
                last.then_inc(outT_done, 1)

            with pe.If(fast):
                def count_blocks(b, ready, free):
                    pe.wait_ge(onehots_ready, ready)
                    if free is not None:
                        pe.wait_ge(counts_staged, free)
                    for i in range(BATCH):
                        for s in range(NS):
                            last = nc.tensor.matmul(blkps[b % 3][:, i, 0:RL], ohS[b % 3][:, i * NS + s, :],
                                                    ohL[b % 3][:, i * NS + s, 0:RL], start=(s == 0), stop=(s == NS - 1))
                    last.then_inc(blocks_done, 1)

                PRIOR = [2, 2, 5, 3, 3]
                for b in range(BPG):
                    count_blocks(b, 2 * (b + 1), b - 2 if b >= 3 else None)
                with pe.Fori(1, NGRP) as g:
                    for b in range(BPG):
                        count_blocks(b, g * (2 * BPG) + 2 * (b + 1), g * BPG + (b - PRIOR[b] + 1))

                def messages(m, j):
                    pe.wait_ge(msg_hi, m)
                    pe.wait_ge(msg_lo, m)
                    node_product(j).then_inc(msg_done, 1)

                def aggregate(j, par, g, k0, k1, first):
                    w = WIDTH[j]
                    for k in range(k0, k1):
                        if first and k % TQ == 0:
                            pe.wait_ge(msg_lo, g + k // TQ + 1)
                        for part in range(2):
                            last = nc.tensor.matmul(psAgg[j % 2][:, 0:w], msgs[:, mpart(par, k, part):mpart(par, k, part) + H],
                                                    adj[:, k * RS + TW * j:k * RS + TW * j + w],
                                                    start=(k == 0 and part == 0), stop=(k == NCH - 1 and part == 1))
                    if k1 == NCH:
                        last.then_inc(agg_done, 1)

                pe.wait_ge(counts_staged, NGRP * BPG)
                for j in range(NT - 2):
                    messages(j, j)
                pe.wait_ge(adj_loaded, 16 * NCH)

                def step(s, par, last):
                    g0 = s * NT
                    K0 = TQ * (NT - 2)
                    pe.wait_ge(aggT_ready, past(g0))
                    aggregate(0, par, g0, 0, K0, True)
                    pe.wait_ge(h_ready, past(g0))
                    messages(g0 + NT - 2, NT - 2)
                    messages(g0 + NT - 1, NT - 1)
                    aggregate(0, par, g0, K0, NCH, True)
                    for j in range(NT):
                        if j < NT - 1:
                            if j >= 1:
                                pe.wait_ge(aggT_ready, past(g0 + j))
                            aggregate(j + 1, par, g0, 0, NCH, False)
                        pe.wait_ge(aggT_ready, past(g0 + j + 1))
                        gru_products(g0 + j, j, aggT[:, 0:WIDTH[j]])
                        if 1 <= j < NT - 1:
                            pe.wait_ge(h_ready, past(g0 + j))
                            if last:
                                if j >= 2:
                                    pe.wait_ge(out_added, j - 1)
                                out_transpose(j - 1)
                            else:
                                messages(g0 + NT + j - 1, j - 1)

                with pe.Fori(0, STEPS - 1, 2) as s:
                    step(s, 0, False)
                    step(s + 1, 1, False)
                step(STEPS - 1, 0, True)
                for j in range(NT - 2, NT):
                    pe.wait_ge(h_ready, past(NT * (STEPS - 1) + j + 1))
                    pe.wait_ge(out_added, j)
                    out_transpose(j)
            with pe.Else():
                with pe.Fori(0, STEPS) as s:
                    pe.wait_ge(h_ready, past(s * NT))
                    for j in range(NT):
                        pe.wait_ge(g_node_ready, past(s * NT + j))
                        node_product(j).then_inc(g_node_sum, 1)
                    pe.wait_ge(g_node_ready, past(s * NT + NT))

                    def edges(u, i, first=False, final=False):
                        pe.wait_ge(g_gathered[i], s * (16 * ET // UN) + 16 * u + 16)
                        pe.wait_ge(g_onehot, s * ET + u * UN + (i + 1))
                        for j in range(NT):
                            last = nc.tensor.matmul(ps[:, j, 0:WIDTH[j]], g_msg[0:125, :],
                                                    g_one[0:125, TW * j:TW * j + WIDTH[j]], start=first, stop=final,
                                                    skip_group_check=True)
                            if final:
                                last.then_inc(agg_done, 1)
                        if not final:
                            last.then_inc(g_tile_done, 1)

                    for i in range(UN):
                        edges(0, i, first=(i == 0))
                    with pe.Fori(1, ET // UN - 1) as u:
                        for i in range(UN):
                            edges(u, i)
                    for i in range(UN):
                        edges(ET // UN - 1, i, final=(i == UN - 1))
                    pe.wait_ge(g_copied, NT * (s + 1))
                    pe.sem_inc(g_tile_done, 1)
                    for j in range(NT):
                        gru_products(s * NT + j, j, g_agg[:, TW * j:TW * j + WIDTH[j]])
                pe.wait_ge(h_ready, past(STEPS * NT))
                for j in range(NT):
                    if j >= 1:
                        pe.wait_ge(out_added, j)
                    out_transpose(j)


_INS = ['x', 'src', 'dst', 'L0_gnn_W_msg', 'L0_gnn_b_msg', 'L0_gnn_W_ih', 'L0_gnn_W_hh', 'L0_gnn_b_ih', 'L0_gnn_b_hh']
_OUTS = [((3125, 128), 'float32')]


def kernel(**inputs):
    import numpy as _np
    import concourse.bacc as _bacc
    from concourse import mybir as _mybir
    from concourse.bass_utils import run_bass_kernel_spmd as _run

    nc = _bacc.Bacc("TRN2", target_bir_lowering=False, num_devices=1)
    arrays, args = {}, []
    for name in _INS:
        a = _np.ascontiguousarray(inputs[name])
        arrays[f"in_{name}_dram"] = a
        args.append(nc.dram_tensor(f"in_{name}_dram", a.shape, _mybir.dt.from_np(a.dtype), kind="ExternalInput").ap())
    for i, (shape, dtype) in enumerate(_OUTS):
        dt = _mybir.dt.from_np(_np.dtype(dtype))
        args.append(nc.dram_tensor(f"out_{i}_dram", shape, dt, kind="ExternalOutput").ap())
    gnn_gated_recurrent_kernel(nc, *args)
    r = _run(nc, [arrays], core_ids=[0])
    got = tuple(r.results[0][f"out_{i}_dram"] for i in range(len(_OUTS)))
    return got[0]
```

```python
import concourse.bass as bass
from concourse import mybir
from contextlib import ExitStack


def gnn_gated_recurrent_kernel(nc, x, src, dst, W_msg, b_msg, W_ih, W_hh, b_ih, b_hh, out):
    f32, f16, i32 = mybir.dt.float32, mybir.dt.float16, mybir.dt.int32
    ALU, ACT, AX = mybir.AluOpType, mybir.ActivationFunctionType, mybir.AxisListType

    N, H = x.shape
    E = src.shape[0]
    STEPS = 5
    P = 128
    NCH = (N + P - 1) // P
    LASTP = N - (NCH - 1) * P
    TW = 512
    NT = (N + TW - 1) // TW
    TQ = TW // P
    RS = N + 1
    WIDTH = [min(TW, N - TW * j) for j in range(NT)]
    CHUNKS = [[(k, min(P, N - P * k)) for k in range(TQ * j, min(TQ * j + TQ, NCH))] for j in range(NT)]

    BLK = 5
    NB = N // BLK
    RH = 25
    RL = N // RH
    SW, LW = 128, RL + 1
    CAP = 256
    NS = CAP // P
    BG = 125
    NG = NB // BG
    SEG = 256
    NSMP = E // SEG
    BATCH = 4
    GRP = 25
    NGRP = NB // GRP
    SIZES = [BATCH] * (GRP // BATCH) + [GRP % BATCH]
    BPG = len(SIZES)
    SLOT = [b % 4 for b in range(BPG)]
    PRIOR = [3, 3, 3, 7, 4, 4, 4]
    LATE = 3
    EARLY = 4
    DIV_MUL, DIV_SHIFT = 4195, 19
    assert N == NB * BLK == RH * RL and NB == NG * BG and BLK * RH == 125
    assert all((r * DIV_MUL) >> DIV_SHIFT == r // RL for r in range(N)) and N * DIV_MUL < 2 ** 24

    ET = E // 125
    UN = 3
    assert ET * 125 == E and ET % UN == 0 and STEPS % 2 == 1

    adj_dram = nc.dram_tensor("adj_scratch", [N, N], f16).ap()
    counts_dram = adj_dram.rearrange("(b c) (h l) -> (c h) b l", c=BLK, l=RL)
    msg_dram = nc.dram_tensor("msg_scratch", [N, H], f32).ap()

    with ExitStack() as ctx:
        def sb(name, shape, dt):
            return ctx.enter_context(nc.sbuf_tensor(name, shape, dt))

        def sem(name):
            return ctx.enter_context(nc.semaphore(name))

        adj = sb("adj", [P, NCH * RS], f16)
        hT = sb("hT", [P, RS], f32)
        msgs = sb("msgs", [P, 2 * NCH * 2 * H], f16)
        work = sb("work", [P, 5, TW], f32)
        aggT, rS, zS, nS, tS = (work[:, i, :] for i in range(5))
        WmT = sb("WmT", [P, H], f32)
        WihT = sb("WihT", [P, 3, H], f32)
        WhhT = sb("WhhT", [P, 3, H], f32)
        ident = sb("ident", [P, P], f32)
        iota = sb("iota", [P, P], f16)
        ones = sb("ones", [1, P], f32)
        ones2 = sb("ones2", [2, P], f16)
        bm2 = sb("bm2", [2, H], f16)
        bhi16 = sb("bhi16", [P, 1], f16)
        bhl = sb("bhl", [P, 2], f32)
        bcol = sb("bcol", [P, 8], f32)
        brz = sb("brz", [P, 2], f32)
        bnd = sb("bnd", [P, 4], f32)
        bndi = bnd[:, :].bitcast(i32)
        flag = sb("flag", [1, 1], i32)
        g_idx = sb("g_idx", [P, 1], i32)
        small = sb("small", [P, 50], f32)
        invs = bnd[:, 3:4]

        early = adj[:, :].bitcast(f32)
        take = [0]

        def carve(n, dt=f32):
            a = early[:, take[0]:take[0] + n]
            take[0] += n
            return a if dt is f32 else a.bitcast(dt)

        xs = carve(NCH * H).rearrange("p (k f) -> p k f", f=H)
        wnat = carve(7 * H).rearrange("p (k f) -> p k f", f=H)
        bnst = carve(NCH * 6).rearrange("p (k s) -> p k s", s=6)
        bnmv = carve(NCH * 2).rearrange("p (k s) -> p k s", s=2)
        lnve, lnsd, lnrs, lnnm = (carve(NCH) for _ in range(4))
        smp_i = carve(NSMP, i32)
        smp_f = carve(NSMP)
        junk = carve(SEG * 2)
        seg_i = carve(NG * SEG, i32).rearrange("p (g e) -> p g e", g=NG)
        seg_f = carve(NG * SEG).rearrange("p (g e) -> p g e", g=NG)
        dst_i = carve(NG * CAP, i32).rearrange("p (g e) -> p g e", g=NG)
        src_i = carve(NG * CAP, i32).rearrange("p (g e) -> p g e", g=NG)
        cl_f = carve(NG * CAP).rearrange("p (g e) -> p g e", g=NG)
        rm_i = carve(NG * CAP, i32).rearrange("p (g e) -> p g e", g=NG)
        rh_i = carve(NG * CAP, i32).rearrange("p (g e) -> p g e", g=NG)
        sk_f = carve(NG * CAP).rearrange("p (g e) -> p g e", g=NG)
        sc_f = carve(NG * CAP).rearrange("p (g e) -> p g e", g=NG)
        lk_f = carve(NG * CAP).rearrange("p (g e) -> p g e", g=NG)
        blk_i = carve(NG, i32)
        off_i = carve(NG, i32)
        start_i = carve(NG, i32)
        blk_f, cnt_a, off_f, cnt_b, start_f = (small[:, 5 * i:5 * i + 5] for i in range(5))
        nlow, nhigh, ndiff, onecol, nval = (small[:, 25 + 5 * i:30 + 5 * i] for i in range(5))
        assert take[0] < (NCH - LATE) * RS // 2

        keys = work[:, :, :].rearrange("p a b -> p (a b)").bitcast(f16)
        skey = keys[:, 0:NB * NS * 2]
        lkey = keys[:, NB * NS * 2:2 * NB * NS * 2]
        OHN = BATCH * NS
        oh_mem = [adj[:, (NCH - LATE) * RS + i * OHN * (SW + LW):] for i in range(4)]
        ohS = [m[:, 0:OHN * SW].rearrange("p (t j) -> p t j", t=OHN) for m in oh_mem]
        ohL = [m[:, OHN * SW:OHN * (SW + LW)].rearrange("p (t j) -> p t j", t=OHN) for m in oh_mem]
        assert 4 * OHN * (SW + LW) <= LATE * RS and 2 * GRP * RL <= NCH * 2 * H
        stage = msgs[:, NCH * 2 * H:NCH * 2 * H + 2 * GRP * RL]

        g_iota = early[:, 0:N]
        g_one = early[:, N:2 * N]
        g_dst = early[:, 2 * N:2 * N + ET].bitcast(i32)
        g_srci = early[:, 2 * N + ET:2 * N + 2 * ET].bitcast(i32)
        g_src = early[:, 2 * N + 2 * ET:2 * N + 3 * ET]
        g_msg = early[:, 7 * ET + 2 * N:7 * ET + 2 * N + H]
        g_agg = early[:, 8 * ET + 2 * N:8 * ET + 3 * N]
        g_node = early[:, 8 * ET + 3 * N:8 * ET + 3 * N + NCH * H]

        ps = ctx.enter_context(nc.psum_tensor("ps", [P, 8, TW], f32))
        psAgg = [ps[:, 0, :], ps[:, 1, :]]
        psR, psZ, psI, psH, psM = (ps[:, i, :] for i in range(2, 7))
        psX = ps[:, 7, :]
        blkps = [ps[:, 2 + i, :].rearrange("p (b j) -> p b j", j=P) for i in range(4)]
        acc0 = [ps[:, 0, :], ps[:, 1, :], ps[:, 7, :], ps[:, 6, :]]
        init_bank = [0, 1, 2, 3, 6, 0, 1]
        g_psA = [ps[:, i, :] for i in range(NT)]

        consts = sem("consts")
        x_padded = sem("x_padded")
        x_loaded = sem("x_loaded")
        w_loaded = sem("w_loaded")
        b_loaded = sem("b_loaded")
        smp_loaded = sem("smp_loaded")
        smp_conv = sem("smp_conv")
        smp_spread = sem("smp_spread")
        coarse_off = sem("coarse_off")
        seg_loaded = sem("seg_loaded")
        fine_off = sem("fine_off")
        win_loaded = [sem(f"win_loaded{g}") for g in range(NG)]
        dv = sem("dv")
        ln_var = sem("ln_var")
        ln_sd = sem("ln_sd")
        ln_scale = sem("ln_scale")
        x_normed = sem("x_normed")
        xT_ready = sem("xT_ready")
        h0_ready = sem("h0_ready")
        wT_ready = sem("wT_ready")
        wT_copied = sem("wT_copied")
        wm_scaled = sem("wm_scaled")
        b_split = sem("b_split")
        dv_msg_pad = sem("dv_msg_pad")
        keys_ready = sem("keys_ready")
        keyT_ready = sem("keyT_ready")
        skey_copied = sem("skey_copied")
        lkey_copied = sem("lkey_copied")
        chunk_summed = sem("chunk_summed")
        msgs_moved = sem("msgs_moved")
        nval_ready = sem("nval_ready")
        nval_summed = sem("nval_summed")
        flag_ready = sem("flag_ready")
        onehots_ready = sem("onehots_ready")
        blocks_done = sem("blocks_done")
        counts_staged = sem("counts_staged")
        stage_written = sem("stage_written")
        adj_loaded = sem("adj_loaded")
        last_cleared = sem("last_cleared")
        agg_done = sem("agg_done")
        aggT_ready = sem("aggT_ready")
        r_summed = sem("r_summed")
        z_summed = sem("z_summed")
        n_summed = sem("n_summed")
        r_ready = sem("r_ready")
        z_ready = sem("z_ready")
        gated = sem("gated")
        n_arg = sem("n_arg")
        n_ready = sem("n_ready")
        h_minus_n = sem("h_minus_n")
        z_times = sem("z_times")
        h_ready = sem("h_ready")
        msg_done = sem("msg_done")
        msg_hi = sem("msg_hi")
        msg_lo = sem("msg_lo")
        x_again = sem("x_again")
        outT_done = sem("outT_done")
        out_added = sem("out_added")
        out_written = sem("out_written")
        g_consts = sem("g_consts")
        g_edges = sem("g_edges")
        g_conv = sem("g_conv")
        g_index = sem("g_index")
        g_node_ready = sem("g_node_ready")
        g_node_sum = sem("g_node_sum")
        g_node_written = sem("g_node_written")
        g_gathered = [sem(f"g_gathered{i}") for i in range(UN)]
        g_onehot = sem("g_onehot")
        g_tile_done = sem("g_tile_done")
        g_copied = sem("g_copied")
        pool_turn = sem("pool_turn")
        sp_turn = sem("sp_turn")
        block = ctx.enter_context(nc.Block())

        def past(n):
            return n + 1

        def mpart(par, k, part):
            return par * (NCH * 2 * H) + (k * 2 + part) * H

        @block.sync
        def _(sp):
            ctx.enter_context(nc.allow_non_contiguous_dma(reason="samples and bias columns: a few hundred single elements"))
            sp.dma_start(smp_i[0:1, :], dst[0:NSMP * SEG].rearrange("(a n s) -> a n s", a=1, s=SEG)[:, :, SEG - 1]
                         ).then_inc(smp_loaded, 16)
            sp.dma_start(xs[:, 0:NCH - 1, :], x[0:(NCH - 1) * P, :].rearrange("(k p) f -> p k f", p=P)
                         ).then_inc(x_loaded, 16)
            sp.wait_ge(x_padded, 1)
            sp.dma_start(xs[0:LASTP, NCH - 1, :], x[(NCH - 1) * P:N, :]).then_inc(x_loaded, 16)
            sp.dma_start(wnat[:, 0, :], W_msg).then_inc(w_loaded, 16)
            sp.dma_start(wnat[:, 1:4, :], W_ih.rearrange("(g p) f -> p g f", p=P)).then_inc(w_loaded, 16)
            sp.dma_start(wnat[:, 4:7, :], W_hh.rearrange("(g p) f -> p g f", p=P)).then_inc(w_loaded, 16)
            sp.dma_start(bcol[:, 0:3], b_ih.rearrange("(g p) -> p g", p=P)).then_inc(b_loaded, 16)
            sp.dma_start(bcol[:, 3:6], b_hh.rearrange("(g p) -> p g", p=P)).then_inc(b_loaded, 16)
            sp.dma_start(bcol[:, 6:7], b_msg.rearrange("(p a) -> p a", a=1)).then_inc(b_loaded, 16)
            def write_counts(g, first):
                sp.wait_ge(counts_staged, BPG * (g + 1))
                sp.sem_inc(sp_turn, 1)
                if not first:
                    sp.wait_ge(stage_written, 32 * g)
                    sp.sem_inc(sp_turn, 1)
                slot = stage[:, bass.ds((g % 2) * (GRP * RL), GRP * RL)].rearrange("p (b j) -> p b j", j=RL)
                to = counts_dram[:, bass.ds(g * GRP, GRP), :]
                sp.dma_start(to[0:120], slot[0:120]).then_inc(stage_written, 16)
                sp.dma_start(to[120:125], slot[120:125]).then_inc(stage_written, 16)

            write_counts(0, True)
            with sp.Fori(1, NGRP) as g:
                write_counts(g, False)
            sp.wait_ge(flag_ready, 1)
            fast = sp.value_load(flag[0:1, 0:1], min_val=0, max_val=1)
            with sp.If(fast):
                sp.wait_ge(msgs_moved, STEPS - 1)
                xres = msgs[:, mpart(1, 0, 0):].bitcast(f32).rearrange("p (k f) -> p k f", f=H)
                sp.dma_start(xres[:, 0:NCH - 1, :], x[0:(NCH - 1) * P, :].rearrange("(k p) f -> p k f", p=P)
                             ).then_inc(x_again, 16)
                sp.dma_start(xres[0:LASTP, NCH - 1, :], x[(NCH - 1) * P:N, :]).then_inc(x_again, 16)
                for j in range(NT):
                    sp.wait_ge(out_added, j + 1)
                    k0, n = CHUNKS[j][0][0], len(CHUNKS[j])
                    if WIDTH[j] == TW:
                        sp.dma_start(out[TW * j:TW * (j + 1), :].rearrange("(k p) f -> p k f", p=P),
                                     xres[:, k0:k0 + n, :]).then_inc(out_written, 16)
                    else:
                        sp.dma_start(out[TW * j:N, :], xres[0:LASTP, k0, :]).then_inc(out_written, 16)
                sp.wait_ge(out_written, 16 * NT)
            with sp.Else():
                sp.wait_ge(chunk_summed, NCH - LATE)
                sp.dma_start(g_dst[0:125, :], dst.rearrange("(p t) -> p t", t=ET)).then_inc(g_edges, 16)
                sp.dma_start(g_srci[0:125, :], src.rearrange("(p t) -> p t", t=ET)).then_inc(g_edges, 16)
                node = g_node.rearrange("p (k f) -> p k f", f=H)
                with sp.Fori(0, STEPS) as s:
                    sp.wait_ge(g_node_ready, past(NT * (s + 1)))
                    sp.sem_inc(sp_turn, 1)
                    sp.dma_start(msg_dram[0:(NCH - 1) * P, :].rearrange("(k p) f -> p k f", p=P),
                                 node[:, 0:NCH - 1, :]).then_inc(g_node_written, 16)
                    sp.dma_start(msg_dram[(NCH - 1) * P:N, :], node[0:LASTP, NCH - 1, :]).then_inc(g_node_written, 16)
                sp.wait_ge(agg_done, past(STEPS * NT))
                sp.wait_ge(h_ready, past(STEPS * NT))
                sp.dma_start(node[:, 0:NCH - 1, :], x[0:(NCH - 1) * P, :].rearrange("(k p) f -> p k f", p=P)
                             ).then_inc(x_again, 16)
                sp.dma_start(node[0:LASTP, NCH - 1, :], x[(NCH - 1) * P:N, :]).then_inc(x_again, 16)
                sp.wait_ge(out_added, NT)
                sp.dma_start(out[0:(NCH - 1) * P, :].rearrange("(k p) f -> p k f", p=P),
                             node[:, 0:NCH - 1, :]).then_inc(out_written, 16)
                sp.dma_start(out[(NCH - 1) * P:N, :], node[0:LASTP, NCH - 1, :]).then_inc(out_written, 16)
                sp.wait_ge(out_written, 32)

        @block.gpsimd
        def _(pool):
            pool.iota(blk_i[0:BG, :], pattern=[[BLK * BG, NG]], base=0, channel_multiplier=BLK).then_inc(consts, 1)
            pool.memset(ident[:, :], 0.0).then_inc(consts, 1)
            pool.memset(ones[:, :], 1.0).then_inc(consts, 1)
            pool.memset(ones2[:, :], 1.0).then_inc(consts, 1)
            pool.wait_ge(consts, 4)
            pool.affine_select(out=ident[:, :], in_=ident[:, :], compare_op=ALU.not_equal, fill=1.0, base=0,
                               pattern=[[-1, P]], channel_multiplier=1).then_inc(consts, 1)
            pool.iota(iota[:, :], pattern=[[1, P]], base=0, channel_multiplier=0,
                      allow_small_or_imprecise_dtypes=True).then_inc(consts, 1)
            flat = [a.rearrange("(a b) -> a b", a=1) for a in (dst, src)]

            def gather(to, g, offsets, of, done):
                pool.indirect_dma_start(out=to[0:BG, g, :], out_offset=None, in_=flat[of],
                                        in_offset=bass.IndirectOffsetOnAxis(ap=offsets[0:BG, g:g + 1], axis=1)
                                        ).then_inc(done, 16)

            pool.wait_ge(coarse_off, 1)
            for g in range(NG):
                gather(seg_i, g, off_i, 0, seg_loaded)
            pool.wait_ge(fine_off, 1)
            for g in range(NG):
                gather(dst_i, g, start_i, 0, win_loaded[g])
                gather(src_i, g, start_i, 1, win_loaded[g])

            def load_chunk(k, groups, rows, first=False):
                pool.wait_ge(stage_written, 32 * groups)
                if not first:
                    pool.wait_ge(adj_loaded, 16 * k)
                pool.dma_start(adj[0:rows, bass.ds(k * RS, N)], adj_dram[bass.ds(k * P, rows), :]
                               ).then_inc(adj_loaded, 16)

            pool.wait_ge(keyT_ready, NG)
            pool.wait_ge(nval_ready, 1)
            load_chunk(0, 2, P, first=True)
            with pool.Fori(1, NCH - LATE) as k:
                load_chunk(k, k + 2, P)
            pool.wait_ge(flag_ready, 1)
            fast = pool.value_load(flag[0:1, 0:1], min_val=0, max_val=1)
            with pool.If(fast):
                pool.wait_ge(last_cleared, 1)
                for k in range(NCH - LATE, NCH):
                    load_chunk(k, NGRP, min(P, N - k * P))
            with pool.Else():
                pool.wait_ge(chunk_summed, NCH - LATE)
                pool.iota(g_iota, pattern=[[1, N]], base=0, channel_multiplier=0,
                          allow_small_or_imprecise_dtypes=True).then_inc(g_consts, 1)
                pool.wait_ge(g_edges, 32)
                with pool.Fori(0, STEPS) as s:
                    pool.wait_ge(g_node_written, 32 * (s + 1))
                    pool.sem_inc(pool_turn, 1)
                    with pool.Fori(0, ET // UN) as u:
                        for i in range(UN):
                            pool.wait_ge(g_index, s * ET + u * UN + (i + 1))
                            pool.sem_inc(pool_turn, 1)
                            pool.indirect_dma_start(
                                out=g_msg[0:125, :], out_offset=None, in_=msg_dram,
                                in_offset=bass.IndirectOffsetOnAxis(ap=g_idx[0:125, :], axis=0)
                            ).then_inc(g_gathered[i], 16)

        @block.vector
        def _(v):
            for started in (n_arg, h_ready, g_node_ready):
                v.sem_inc(started, 1)
            chain = [0]

            def link(ins):
                chain[0] += 1
                ins.then_inc(dv, 1)
                v.wait_ge(dv, chain[0])

            nc.vector.memset(xs[0:P, NCH - 1, :], 0.0).then_inc(x_padded, 1)
            link(nc.vector.memset(small[:, :], 0.0))
            link(nc.vector.memset(onecol[:, :], 1.0))
            v.wait_ge(smp_loaded, 16)
            nc.vector.tensor_copy(smp_f[0:1, :], smp_i[0:1, :]).then_inc(smp_conv, 1)
            v.wait_ge(consts, 6)
            link(nc.vector.tensor_copy(blk_f[0:BG, :], blk_i[0:BG, :]))
            v.wait_ge(smp_spread, 1)
            for g in range(NG):
                link(nc.vector.tensor_scalar(junk[0:BG, 0:NSMP], psX[0:BG, 0:NSMP], blk_f[0:BG, g:g + 1], None,
                                             ALU.is_lt, op1=ALU.add, accum_out=cnt_a[0:BG, g:g + 1]))
            link(nc.vector.tensor_scalar(off_f[0:BG, :], cnt_a[0:BG, :], float(SEG), float(E - SEG), ALU.mult, ALU.min))
            nc.vector.tensor_copy(off_i[0:BG, :], off_f[0:BG, :]).then_inc(coarse_off, 1)
            v.wait_ge(x_loaded, 32)
            for k in range(NCH):
                nc.vector.bn_stats(bnst[:, k, :], xs[:, k, :]).then_inc(dv, 1)
            chain[0] += NCH
            v.wait_ge(dv, chain[0])
            for k in range(NCH):
                nc.vector.bn_aggr(bnmv[:, k, :], bnst[:, k, :]).then_inc(dv, 1)
            chain[0] += NCH
            v.wait_ge(dv, chain[0])
            nc.vector.tensor_scalar(lnve, bnmv[:, :, 1], 1e-5, None, ALU.add).then_inc(ln_var, 1)
            v.wait_ge(seg_loaded, 16 * NG)
            link(nc.vector.tensor_copy(seg_f[0:BG], seg_i[0:BG]))
            for g in range(NG):
                link(nc.vector.tensor_scalar(junk[0:BG, 0:SEG], seg_f[0:BG, g, :], blk_f[0:BG, g:g + 1], None,
                                             ALU.is_lt, op1=ALU.add, accum_out=cnt_b[0:BG, g:g + 1]))
            link(nc.vector.tensor_tensor(start_f[0:BG, :], off_f[0:BG, :], cnt_b[0:BG, :], ALU.add))
            nc.vector.tensor_scalar(start_i[0:BG, :], start_f[0:BG, :], float(E - CAP), None, ALU.min
                                    ).then_inc(fine_off, 1)
            v.wait_ge(ln_sd, 1)
            link(nc.vector.reciprocal(lnrs, lnsd))
            nc.vector.scalar_tensor_tensor(out=lnnm, in0=bnmv[:, :, 0], scalar=-1.0, in1=lnrs,
                                           op0=ALU.mult, op1=ALU.mult).then_inc(ln_scale, 1)
            v.wait_ge(w_loaded, 48)
            v.wait_ge(b_loaded, 48)
            link(nc.vector.tensor_reduce(bnd[:, 0:1], wnat[:, 0, :], AX.X, ALU.add, apply_absolute_value=True))
            link(nc.vector.tensor_scalar(bcol[:, 7:8].bitcast(i32), bcol[:, 6:7].bitcast(i32), 0x7FFFFFFF, None,
                                         ALU.bitwise_and))
            link(nc.vector.tensor_scalar(bnd[:, 1:2], bnd[:, 0:1], 12.0, 1e-30, ALU.mult, ALU.add))
            link(nc.vector.tensor_tensor(bnd[:, 0:1], bnd[:, 1:2], bcol[:, 7:8], ALU.add))
            link(nc.vector.tensor_scalar(bndi[:, 1:2], bndi[:, 0:1], 0x7F800000, None, ALU.bitwise_and))
            link(nc.vector.tensor_scalar(bndi[:, 2:3], bndi[:, 1:2], 0x7F800000, None, ALU.bitwise_xor))
            link(nc.vector.tensor_scalar(bnd[:, 2:3], bnd[:, 2:3], float(2 ** 13), None, ALU.mult))
            nc.vector.tensor_scalar(wnat[:, 0, :], wnat[:, 0, :], bnd[:, 2:3], None, ALU.mult).then_inc(wm_scaled, 1)
            link(nc.vector.tensor_scalar(bnd[:, 3:4], bnd[:, 1:2], float(2 ** -14), None, ALU.mult))
            link(nc.vector.tensor_tensor(brz[:, :], bcol[:, 0:2], bcol[:, 3:5], ALU.add))
            link(nc.vector.tensor_scalar(bcol[:, 7:8], bcol[:, 6:7], bnd[:, 2:3], None, ALU.mult))
            link(nc.vector.tensor_copy(bhi16[:, :], bcol[:, 7:8]))
            link(nc.vector.tensor_copy(bhl[:, 0:1], bhi16[:, :]))
            nc.vector.tensor_tensor(bhl[:, 1:2], bcol[:, 7:8], bhi16[:, :], ALU.subtract).then_inc(b_split, 1)
            nc.vector.memset(msgs[:, mpart(0, NCH - 1, 0):mpart(0, NCH - 1, 2)], 0.0).then_inc(dv_msg_pad, 1)

            def lo_part(m, par, j, bank=6):
                v.wait_ge(msg_hi, m + 1)
                rows, n, k0 = CHUNKS[j][-1][1], len(CHUNKS[j]), CHUNKS[j][0][0]
                tile = msgs[0:rows, mpart(par, k0, 0):mpart(par, k0 + n, 0)].rearrange("p (k a f) -> p k a f", a=2, f=H)
                nc.vector.tensor_tensor(tile[:, :, 1, :], ps[0:rows, bank, 0:n * H].rearrange("p (k f) -> p k f", f=H),
                                        tile[:, :, 0, :], ALU.subtract).then_inc(msg_lo, 1)

            def edge_keys(g):
                v.wait_ge(win_loaded[g], 32)
                nc.vector.tensor_scalar(rm_i[0:BG, g], src_i[0:BG, g], float(DIV_MUL), None, ALU.mult).then_inc(dv, 1)
                nc.vector.tensor_scalar(cl_f[0:BG, g], dst_i[0:BG, g], blk_f[0:BG, g:g + 1], None, ALU.subtract
                                        ).then_inc(dv, 1)
                chain[0] += 2
                v.wait_ge(dv, chain[0])
                link(nc.vector.tensor_scalar(rh_i[0:BG, g], rm_i[0:BG, g], DIV_SHIFT, None, ALU.logical_shift_right))
                link(nc.vector.scalar_tensor_tensor(out=sk_f[0:BG, g], in0=cl_f[0:BG, g], scalar=float(RH),
                                                    in1=rh_i[0:BG, g], op0=ALU.mult, op1=ALU.add))
                link(nc.vector.tensor_scalar(sc_f[0:BG, g], sk_f[0:BG, g], -1.0, 255.0, ALU.max, ALU.min))
                nc.vector.scalar_tensor_tensor(out=lk_f[0:BG, g], in0=rh_i[0:BG, g], scalar=float(-RL),
                                               in1=src_i[0:BG, g], op0=ALU.mult, op1=ALU.add).then_inc(keys_ready, 1)
                nc.vector.tensor_scalar(seg_f[0:BG, g], cl_f[0:BG, g], float(BLK), None, ALU.is_lt, op1=ALU.add,
                                        accum_out=nlow[0:BG, g:g + 1]).then_inc(dv, 1)
                nc.vector.tensor_scalar(junk[0:BG, 0:CAP], cl_f[0:BG, g], 0.0, None, ALU.is_lt, op1=ALU.add,
                                        accum_out=nhigh[0:BG, g:g + 1]).then_inc(dv, 1)
                chain[0] += 2

            def copy_skey(g):
                v.wait_ge(keyT_ready, g + 1)
                nc.vector.tensor_copy(
                    skey.rearrange("p (b s d) -> p b s d", s=NS, d=2)[:, BG * g:BG * (g + 1)],
                    ps[:, 4, 0:NS * P].rearrange("p (s b d) -> p b s d", s=NS, d=1)[:, 0:BG]
                    .broadcast_to([P, BG, NS, 2])).then_inc(skey_copied, 1)

            for g in range(NG):
                edge_keys(g)
                if g >= 1:
                    copy_skey(g - 1)
                lo_part(g, 0, g, init_bank[g])
            copy_skey(NG - 1)
            for j in range(NG, NT):
                lo_part(j, 0, j, init_bank[j])
            v.wait_ge(dv, chain[0])
            link(nc.vector.tensor_tensor(ndiff[:, :], nlow[:, :], nhigh[:, :], ALU.subtract))
            nc.vector.tensor_reduce(nval[:, 0:1], ndiff[:, :], AX.X, ALU.add).then_inc(nval_ready, 1)
            v.wait_ge(nval_summed, 1)
            nc.vector.tensor_scalar(flag[0:1, 0:1], psX[0:1, 0:1], float(E), None, ALU.is_equal).then_inc(flag_ready, 1)

            def onehots(b, kcol, prior):
                if prior is not None:
                    v.wait_ge(blocks_done, prior)
                n = SIZES[b] * NS
                for oh, key, w in ((ohS, skey, SW), (ohL, lkey, LW)):
                    k4 = key[:, bass.ds(kcol, n * 2)].rearrange("p (t o d) -> p t o d", o=1, d=2)
                    i4 = iota[:, 0:w].rearrange("p (o j d) -> p o j d", o=1, d=2)
                    shape = [P, n, w // 2, 2]
                    nc.vector.tensor_tensor(oh[SLOT[b]][:, 0:n].rearrange("p t (j d) -> p t j d", d=2),
                                            k4.broadcast_to(shape), i4.broadcast_to(shape), ALU.is_equal
                                            ).then_inc(onehots_ready, 1)

            v.wait_ge(lkey_copied, NG)
            for b in range(BPG):
                onehots(b, b * OHN * 2, b - 3 if b >= 4 else None)
            with v.Fori(1, NGRP) as g:
                for b in range(BPG):
                    onehots(b, g * (GRP * NS * 2) + b * OHN * 2, g * BPG + (b - PRIOR[b] + 1))
            v.wait_ge(flag_ready, 1)
            fast = v.value_load(flag[0:1, 0:1], min_val=0, max_val=1)

            def gates(g, cols, w):
                v.wait_ge(r_ready, past(g + 1))
                v.wait_ge(n_summed, g + 1)
                v.wait_ge(n_ready, past(g))
                nc.vector.scalar_tensor_tensor(out=tS[:, 0:w], in0=psH[:, 0:w], scalar=bcol[:, 5:6], in1=rS[:, 0:w],
                                               op0=ALU.add, op1=ALU.mult).then_inc(gated, 1)
                v.wait_ge(gated, g + 1)
                nc.vector.tensor_tensor(tS[:, 0:w], psI[:, 0:w], tS[:, 0:w], ALU.add).then_inc(n_arg, 1)
                v.wait_ge(n_ready, past(g + 1))
                h = hT[:, cols:cols + w]
                nc.vector.tensor_tensor(rS[:, 0:w], h, nS[:, 0:w], ALU.subtract).then_inc(h_minus_n, 1)
                v.wait_ge(h_minus_n, g + 1)
                v.wait_ge(z_ready, past(g + 1))
                nc.vector.tensor_tensor(rS[:, 0:w], rS[:, 0:w], zS[:, 0:w], ALU.mult).then_inc(z_times, 1)
                v.wait_ge(z_times, g + 1)
                nc.vector.tensor_tensor(h, rS[:, 0:w], nS[:, 0:w], ALU.add).then_inc(h_ready, 1)

            with v.If(fast):
                v.wait_ge(blocks_done, NGRP * BPG)
                nc.vector.memset(adj[:, (NCH - 1) * RS:NCH * RS], 0.0).then_inc(last_cleared, 1)
                v.wait_ge(stage_written, 32 * NGRP)

                def move_messages(s):
                    v.wait_ge(agg_done, past(NT * (s + 1)))
                    v.wait_ge(msg_lo, NT * (s + 1) + EARLY)
                    nc.vector.tensor_copy(msgs[:, mpart(0, 0, 0):mpart(0, TQ * EARLY, 0)],
                                          msgs[:, mpart(1, 0, 0):mpart(1, TQ * EARLY, 0)]).then_inc(msgs_moved, 1)

                def first_step():
                    for j in range(EARLY):
                        gates(j, TW * j, TW)
                    lo_part(NT, 1, 0)
                    lo_part(NT + 1, 1, 1)
                    gates(EARLY, TW * EARLY, TW)
                    lo_part(NT + 2, 1, 2)
                    gates(EARLY + 1, TW * (EARLY + 1), TW)
                    lo_part(NT + 3, 1, 3)
                    move_messages(0)
                    lo_part(NT + 4, 0, 4)
                    gates(NT - 1, TW * (NT - 1), WIDTH[NT - 1])

                def step(s, last):
                    g0 = s * NT
                    lo_part(g0 + NT - 2, 0, NT - 2)
                    lo_part(g0 + NT - 1, 0, NT - 1)
                    for j in range(NT):
                        gates(g0 + j, TW * j, WIDTH[j])
                        if last:
                            if j >= 1:
                                add_x(j - 1)
                        elif 1 <= j <= EARLY:
                            lo_part(g0 + NT + j - 1, 1, j - 1)
                            if j == EARLY:
                                move_messages(s)
                        elif j == NT - 2:
                            lo_part(g0 + NT + j - 1, 0, j - 1)
                    if last:
                        add_x(NT - 1)

                xres = msgs[:, mpart(1, 0, 0):].bitcast(f32).rearrange("p (k f) -> p k f", f=H)

                def add_x(j):
                    v.wait_ge(outT_done, j + 1)
                    if j == 0:
                        v.wait_ge(x_again, 32)
                    rows, n, k0 = CHUNKS[j][-1][1], len(CHUNKS[j]), CHUNKS[j][0][0]
                    nc.vector.tensor_tensor(xres[0:rows, k0:k0 + n, :],
                                            psM[0:rows, 0:n * H].rearrange("p (k f) -> p k f", f=H),
                                            xres[0:rows, k0:k0 + n, :], ALU.add).then_inc(out_added, 1)

                first_step()
                with v.Fori(1, STEPS - 1) as s:
                    step(s, False)
                step(STEPS - 1, True)
            with v.Else():
                v.wait_ge(g_edges, 32)
                nc.vector.tensor_copy(g_src[0:125, :], g_srci[0:125, :]).then_inc(g_conv, 1)
                v.wait_ge(g_conv, 1)
                v.wait_ge(g_consts, 1)
                node = g_node.rearrange("p (k f) -> p k f", f=H)
                with v.Fori(0, STEPS) as s:
                    for j in range(NT):
                        rows, n, k0 = CHUNKS[j][-1][1], len(CHUNKS[j]), CHUNKS[j][0][0]
                        v.wait_ge(g_node_sum, s * NT + j + 1)
                        v.wait_ge(agg_done, past(NT * s))
                        nc.vector.tensor_copy(node[0:rows, k0:k0 + n, :],
                                              psM[0:rows, 0:n * H].rearrange("p (k f) -> p k f", f=H)
                                              ).then_inc(g_node_ready, 1)
                    with v.Fori(0, ET) as t:
                        v.wait_ge(g_tile_done, past(s * ET + t))
                        nc.vector.tensor_copy(g_idx[0:125, :], g_dst[0:125, bass.ds(t, 1)]).then_inc(g_index, 1)
                        nc.vector.tensor_scalar(g_one[0:125, :], g_iota[0:125, :], g_src[0:125, bass.ds(t, 1)], None,
                                                ALU.is_equal).then_inc(g_onehot, 1)
                    v.wait_ge(agg_done, past(NT * (s + 1)))
                    for j in range(NT):
                        nc.vector.tensor_scalar(g_agg[:, TW * j:TW * j + WIDTH[j]], ps[:, j, 0:WIDTH[j]], invs, None,
                                                ALU.mult).then_inc(g_copied, 1)
                    for j in range(NT):
                        gates(s * NT + j, TW * j, WIDTH[j])
                v.wait_ge(x_again, 32)
                for j in range(NT):
                    rows, n, k0 = CHUNKS[j][-1][1], len(CHUNKS[j]), CHUNKS[j][0][0]
                    v.wait_ge(outT_done, j + 1)
                    nc.vector.tensor_tensor(node[0:rows, k0:k0 + n, :],
                                            psM[0:rows, 0:n * H].rearrange("p (k f) -> p k f", f=H),
                                            node[0:rows, k0:k0 + n, :], ALU.add).then_inc(out_added, 1)

        @block.scalar
        def _(act):
            for started in (r_ready, z_ready, n_ready, aggT_ready):
                act.sem_inc(started, 1)
            act.wait_ge(ln_var, 1)
            nc.scalar.activation(lnsd, lnve, ACT.Sqrt).then_inc(ln_sd, 1)
            act.wait_ge(ln_scale, 1)
            for k in range(NCH):
                nc.scalar.activation(xs[:, k, :], xs[:, k, :], ACT.Relu, bias=lnnm[:, k:k + 1],
                                     scale=lnrs[:, k:k + 1]).then_inc(x_normed, 1)
            act.wait_ge(wT_ready, 1)
            nc.scalar.activation(WmT[:, :], ps[:, 0, 0:P], ACT.Copy).then_inc(wT_copied, 1)
            nc.scalar.activation(WihT[:, :, :], ps[:, 0, P:4 * P].rearrange("p (g f) -> p g f", g=3), ACT.Copy
                                 ).then_inc(wT_copied, 1)
            nc.scalar.activation(WhhT[:, :, :], ps[:, 1, 0:3 * P].rearrange("p (g f) -> p g f", g=3), ACT.Copy
                                 ).then_inc(wT_copied, 1)
            nc.scalar.activation(bm2[:, :], ps[0:2, 1, 3 * P:4 * P], ACT.Copy).then_inc(wT_copied, 1)
            for j in range(NT):
                act.wait_ge(xT_ready, j + 1)
                nc.scalar.activation(hT[:, TW * j:TW * j + WIDTH[j]], ps[:, 2 + j % 2, 0:WIDTH[j]], ACT.Copy
                                     ).then_inc(h0_ready, 1)

            def hi_part(m, par, j, bank=6):
                act.wait_ge(msg_done, m + 1)
                rows, n, k0 = CHUNKS[j][-1][1], len(CHUNKS[j]), CHUNKS[j][0][0]
                tile = msgs[0:rows, mpart(par, k0, 0):mpart(par, k0 + n, 0)].rearrange("p (k a f) -> p k a f", a=2, f=H)
                nc.scalar.activation(tile[:, :, 0, :], ps[0:rows, bank, 0:n * H].rearrange("p (k f) -> p k f", f=H),
                                     ACT.Copy).then_inc(msg_hi, 1)

            def copy_lkey(g):
                act.wait_ge(keyT_ready, g + 1)
                nc.scalar.activation(
                    lkey.rearrange("p (b s d) -> p b s d", s=NS, d=2)[:, BG * g:BG * (g + 1)],
                    ps[:, 5, 0:NS * P].rearrange("p (s b d) -> p b s d", s=NS, d=1)[:, 0:BG]
                    .broadcast_to([P, BG, NS, 2]), ACT.Copy).then_inc(lkey_copied, 1)

            act.wait_ge(dv_msg_pad, 1)
            for j in range(NG):
                hi_part(j, 0, j, init_bank[j])
            for g in range(NG):
                copy_lkey(g)
                if g in (1, 2):
                    hi_part(NG + g - 1, 0, NG + g - 1, init_bank[NG + g - 1])

            def stage_batch(b, col, ready, free):
                act.wait_ge(blocks_done, ready)
                if free is not None:
                    act.wait_ge(stage_written, free)
                nc.scalar.activation(stage[0:125, bass.ds(col, SIZES[b] * RL)].rearrange("p (b j) -> p b j", j=RL),
                                     blkps[SLOT[b]][0:125, 0:SIZES[b], 0:RL], ACT.Copy).then_inc(counts_staged, 1)

            for g in range(2):
                for b in range(BPG):
                    stage_batch(b, (g * GRP + b * BATCH) * RL, g * BPG + b + 1, None)
            with act.Fori(2, NGRP) as g:
                for b in range(BPG):
                    stage_batch(b, (g % 2) * (GRP * RL) + b * BATCH * RL, g * BPG + b + 1,
                                32 * (g - 1) if b == 0 else None)
            act.wait_ge(flag_ready, 1)
            fast = act.value_load(flag[0:1, 0:1], min_val=0, max_val=1)

            def gates(g, w):
                act.wait_ge(r_summed, g + 1)
                act.wait_ge(h_ready, past(g))
                nc.scalar.activation(rS[:, 0:w], psR[:, 0:w], ACT.Sigmoid, bias=brz[:, 0:1]).then_inc(r_ready, 1)
                act.wait_ge(z_summed, past(g + 1))
                nc.scalar.activation(zS[:, 0:w], psZ[:, 0:w], ACT.Sigmoid, bias=brz[:, 1:2]).then_inc(z_ready, 1)
                act.wait_ge(n_arg, past(g + 1))
                nc.scalar.activation(nS[:, 0:w], tS[:, 0:w], ACT.Tanh, bias=bcol[:, 2:3]).then_inc(n_ready, 1)

            with act.If(fast):
                def evac(g, w, bank):
                    act.wait_ge(agg_done, past(g + 1))
                    act.wait_ge(z_summed, past(g))
                    nc.scalar.activation(aggT[:, 0:w], bank[:, 0:w], ACT.Identity, scale=invs
                                         ).then_inc(aggT_ready, 1)

                act.wait_ge(stage_written, 32 * NGRP)

                def first_step():
                    for j in range(EARLY):
                        evac(j, TW, acc0[j])
                        gates(j, TW)
                    evac(EARLY, TW, psAgg[0])
                    hi_part(NT, 1, 0)
                    hi_part(NT + 1, 1, 1)
                    gates(EARLY, TW)
                    evac(EARLY + 1, TW, psAgg[1])
                    hi_part(NT + 2, 1, 2)
                    gates(EARLY + 1, TW)
                    evac(NT - 1, WIDTH[NT - 1], psAgg[0])
                    hi_part(NT + 3, 1, 3)
                    hi_part(NT + 4, 0, 4)
                    gates(NT - 1, WIDTH[NT - 1])

                def step(s, last):
                    g0 = s * NT
                    hi_part(g0 + NT - 2, 0, NT - 2)
                    hi_part(g0 + NT - 1, 0, NT - 1)
                    evac(g0, TW, psAgg[0])
                    for j in range(NT):
                        if j < NT - 1:
                            evac(g0 + j + 1, WIDTH[j + 1], psAgg[(j + 1) % 2])
                        gates(g0 + j, WIDTH[j])
                        if not last and 1 <= j < NT - 1:
                            hi_part(g0 + NT + j - 1, 1 if j <= EARLY else 0, j - 1)

                first_step()
                with act.Fori(1, STEPS - 1) as s:
                    step(s, False)
                step(STEPS - 1, True)
            with act.Else():
                with act.Fori(0, STEPS) as s:
                    for j in range(NT):
                        gates(s * NT + j, WIDTH[j])

        @block.tensor
        def _(pe):
            for started in (z_summed, agg_done, g_tile_done):
                pe.sem_inc(started, 1)
            pe.wait_ge(smp_conv, 1)
            pe.wait_ge(consts, 6)
            nc.tensor.matmul(psX[0:BG, 0:NSMP], ones[0:1, 0:BG], smp_f[0:1, :], start=True, stop=True
                             ).then_inc(smp_spread, 1)
            pe.wait_ge(wm_scaled, 1)
            for i in range(7):
                nc.tensor.transpose(ps[:, i // 4, (i % 4) * P:(i % 4 + 1) * P], wnat[:, i, :], ident[:, :])
            pe.wait_ge(b_split, 1)
            nc.tensor.matmul(ps[0:2, 1, 3 * P:4 * P], bhl[:, :], ident[:, :], start=True, stop=True
                             ).then_inc(wT_ready, 1)
            for j in range(NT):
                pe.wait_ge(x_normed, CHUNKS[j][-1][0] + 1)
                if j >= 2:
                    pe.wait_ge(h0_ready, j - 1)
                for k, rows in CHUNKS[j]:
                    last = nc.tensor.transpose(ps[:, 2 + j % 2, (k % TQ) * P:(k % TQ) * P + rows], xs[0:rows, k, :],
                                               ident[0:rows, 0:rows])
                last.then_inc(xT_ready, 1)

            def node_product(j, bank=6):
                for k, rows in CHUNKS[j]:
                    to = ps[0:rows, bank, (k % TQ) * H:(k % TQ + 1) * H]
                    nc.tensor.matmul(to, hT[:, P * k:P * k + rows], WmT[:, :], start=True, stop=False)
                    last = nc.tensor.matmul(to, ones2[0:2, 0:rows], bm2[0:2, :], start=False, stop=True)
                return last

            def edge_key_transposes(g):
                pe.wait_ge(keys_ready, g + 1)
                if g >= 1:
                    pe.wait_ge(skey_copied, g)
                    pe.wait_ge(lkey_copied, g)
                for bank, key in ((4, sc_f), (5, lk_f)):
                    for t in range(NS):
                        last = nc.tensor.transpose(ps[:, bank, t * P:t * P + BG], key[0:BG, g, t * P:(t + 1) * P],
                                                   ident[0:BG, 0:BG])
                last.then_inc(keyT_ready, 1)

            pe.wait_ge(wT_copied, 4)
            pe.wait_ge(h0_ready, NT)
            for j in range(NG):
                node_product(j, init_bank[j]).then_inc(msg_done, 1)
            for g in range(NG):
                edge_key_transposes(g)
                if g in (1, 2):
                    j = NG + g - 1
                    pe.wait_ge(msg_lo, g)
                    node_product(j, init_bank[j]).then_inc(msg_done, 1)
            pe.wait_ge(nval_ready, 1)
            nc.tensor.matmul(psX[0:1, 0:1], nval[0:BG, 0:1], onecol[0:BG, 0:1], start=True, stop=True
                             ).then_inc(nval_summed, 1)
            pe.wait_ge(msg_lo, NT)
            pe.wait_ge(skey_copied, NG)
            pe.wait_ge(lkey_copied, NG)

            def count_blocks(b, ready, free):
                pe.wait_ge(onehots_ready, ready)
                if free is not None:
                    pe.wait_ge(counts_staged, free)
                for i in range(SIZES[b]):
                    for t in range(NS):
                        last = nc.tensor.matmul(blkps[SLOT[b]][:, i, 0:RL], ohS[SLOT[b]][:, i * NS + t, :],
                                                ohL[SLOT[b]][:, i * NS + t, 0:RL], start=(t == 0), stop=(t == NS - 1),
                                                skip_group_check=True)
                last.then_inc(blocks_done, 1)

            def count_group(g):
                for b in range(BPG):
                    if isinstance(g, int) and g == 0:
                        count_blocks(b, 2 * (b + 1), b - 3 if b >= 4 else None)
                    else:
                        count_blocks(b, g * (2 * BPG) + 2 * (b + 1), g * BPG + (b - PRIOR[b] + 1))

            def sum_chunk(k, start):
                pe.wait_ge(adj_loaded, 16 * k + 16)
                for part in range(2):
                    for j in range(EARLY):
                        last = nc.tensor.matmul(acc0[j], msgs[:, bass.ds(mpart(0, k, part), H)],
                                                adj[:, bass.ds(k * RS + TW * j, TW)], start=start and part == 0,
                                                stop=False, skip_group_check=True)
                last.then_inc(chunk_summed, 1)

            count_group(0)
            with pe.Fori(1, LATE) as g:
                count_group(g)
            pe.wait_ge(flag_ready, 1)
            count_group(LATE)
            sum_chunk(0, True)
            with pe.Fori(LATE + 1, NGRP) as g:
                count_group(g)
                sum_chunk(g - LATE, False)
            fast = pe.value_load(flag[0:1, 0:1], min_val=0, max_val=1)

            def gru_products(g, j, src_agg):
                w = WIDTH[j]
                h = hT[:, TW * j:TW * j + w]
                pe.wait_ge(r_ready, past(g))
                nc.tensor.matmul(psR[:, 0:w], WhhT[:, 0, :], h, start=True, stop=False)
                nc.tensor.matmul(psR[:, 0:w], WihT[:, 0, :], src_agg, start=False, stop=True).then_inc(r_summed, 1)
                pe.wait_ge(n_arg, past(g))
                nc.tensor.matmul(psH[:, 0:w], WhhT[:, 2, :], h, start=True, stop=True)
                nc.tensor.matmul(psI[:, 0:w], WihT[:, 2, :], src_agg, start=True, stop=True).then_inc(n_summed, 1)
                pe.wait_ge(z_ready, past(g))
                nc.tensor.matmul(psZ[:, 0:w], WhhT[:, 1, :], h, start=True, stop=False)
                nc.tensor.matmul(psZ[:, 0:w], WihT[:, 1, :], src_agg, start=False, stop=True).then_inc(z_summed, 1)

            def out_transpose(j):
                for k, rows in CHUNKS[j]:
                    last = nc.tensor.transpose(psM[0:rows, (k % TQ) * H:(k % TQ + 1) * H], hT[:, P * k:P * k + rows],
                                               ident[:, :])
                last.then_inc(outT_done, 1)

            with pe.If(fast):
                def messages(m, j):
                    pe.wait_ge(msg_hi, m)
                    pe.wait_ge(msg_lo, m)
                    node_product(j).then_inc(msg_done, 1)

                def aggregate(j, k0, k1, waits={}):
                    w = WIDTH[j]
                    for k in range(k0, k1):
                        if k in waits:
                            pe.wait_ge(msg_lo, waits[k])
                        for part in range(2):
                            last = nc.tensor.matmul(psAgg[j % 2][:, 0:w], msgs[:, mpart(0, k, part):mpart(0, k, part) + H],
                                                    adj[:, k * RS + TW * j:k * RS + TW * j + w],
                                                    start=(k == 0 and part == 0), stop=(k == NCH - 1 and part == 1))
                    if k1 == NCH:
                        last.then_inc(agg_done, 1)

                def gru(g, j):
                    pe.wait_ge(aggT_ready, past(g + 1))
                    gru_products(g, j, aggT[:, 0:WIDTH[j]])

                def first_step():
                    for j in range(EARLY):
                        for k in range(NCH - LATE, NCH):
                            if j == 0:
                                pe.wait_ge(adj_loaded, 16 * (k + 1))
                            for part in range(2):
                                last = nc.tensor.matmul(acc0[j], msgs[:, mpart(0, k, part):mpart(0, k, part) + H],
                                                        adj[:, k * RS + TW * j:k * RS + TW * (j + 1)], start=False,
                                                        stop=(k == NCH - 1 and part == 1), skip_group_check=True)
                        last.then_inc(agg_done, 1)
                    gru(0, 0)
                    aggregate(EARLY, 0, NCH)
                    gru(1, 1)
                    aggregate(EARLY + 1, 0, NCH)
                    gru(2, 2)
                    gru(3, 3)
                    pe.wait_ge(aggT_ready, past(EARLY + 1))
                    aggregate(NT - 1, 0, NCH)
                    pe.wait_ge(h_ready, past(2))
                    messages(NT, 0)
                    messages(NT + 1, 1)
                    gru(4, 4)
                    pe.wait_ge(h_ready, past(3))
                    messages(NT + 2, 2)
                    gru(5, 5)
                    pe.wait_ge(h_ready, past(5))
                    messages(NT + 3, 3)
                    messages(NT + 4, 4)
                    gru(6, 6)

                def step(s, last):
                    g0 = s * NT
                    K0 = TQ * (NT - 2)
                    pe.wait_ge(aggT_ready, past(g0))
                    pe.wait_ge(msgs_moved, s)
                    aggregate(0, 0, K0, {TQ * EARLY: g0 + EARLY + 1})
                    pe.wait_ge(h_ready, past(g0))
                    messages(g0 + NT - 2, NT - 2)
                    messages(g0 + NT - 1, NT - 1)
                    aggregate(0, K0, NCH, {K0: g0 + NT - 1, K0 + TQ: g0 + NT})
                    for j in range(NT):
                        if j < NT - 1:
                            if j >= 1:
                                pe.wait_ge(aggT_ready, past(g0 + j))
                            aggregate(j + 1, 0, NCH)
                        gru(g0 + j, j)
                        if 1 <= j < NT - 1:
                            pe.wait_ge(h_ready, past(g0 + j))
                            if last:
                                if j >= 2:
                                    pe.wait_ge(out_added, j - 1)
                                out_transpose(j - 1)
                            else:
                                messages(g0 + NT + j - 1, j - 1)

                first_step()
                with pe.Fori(1, STEPS - 1) as s:
                    step(s, False)
                step(STEPS - 1, True)
                for j in range(NT - 2, NT):
                    pe.wait_ge(h_ready, past(NT * (STEPS - 1) + j + 1))
                    pe.wait_ge(out_added, j)
                    out_transpose(j)
            with pe.Else():
                with pe.Fori(0, STEPS) as s:
                    pe.wait_ge(h_ready, past(s * NT))
                    for j in range(NT):
                        pe.wait_ge(g_node_ready, past(s * NT + j))
                        node_product(j).then_inc(g_node_sum, 1)
                    pe.wait_ge(g_node_ready, past(s * NT + NT))

                    def edges(u, i, first=False, final=False):
                        pe.wait_ge(g_gathered[i], s * (16 * ET // UN) + 16 * u + 16)
                        pe.wait_ge(g_onehot, s * ET + u * UN + (i + 1))
                        for j in range(NT):
                            last = nc.tensor.matmul(ps[:, j, 0:WIDTH[j]], g_msg[0:125, :],
                                                    g_one[0:125, TW * j:TW * j + WIDTH[j]], start=first, stop=final,
                                                    skip_group_check=True)
                            if final:
                                last.then_inc(agg_done, 1)
                        if not final:
                            last.then_inc(g_tile_done, 1)

                    for i in range(UN):
                        edges(0, i, first=(i == 0))
                    with pe.Fori(1, ET // UN - 1) as u:
                        for i in range(UN):
                            edges(u, i)
                    for i in range(UN):
                        edges(ET // UN - 1, i, final=(i == UN - 1))
                    pe.wait_ge(g_copied, NT * (s + 1))
                    pe.sem_inc(g_tile_done, 1)
                    for j in range(NT):
                        gru_products(s * NT + j, j, g_agg[:, TW * j:TW * j + WIDTH[j]])
                pe.wait_ge(h_ready, past(STEPS * NT))
                for j in range(NT):
                    if j >= 1:
                        pe.wait_ge(out_added, j)
                    out_transpose(j)


_INS = ['x', 'src', 'dst', 'L0_gnn_W_msg', 'L0_gnn_b_msg', 'L0_gnn_W_ih', 'L0_gnn_W_hh', 'L0_gnn_b_ih', 'L0_gnn_b_hh']
_OUTS = [((3125, 128), 'float32')]


def kernel(**inputs):
    import numpy as _np
    import concourse.bacc as _bacc
    from concourse import mybir as _mybir
    from concourse.bass_utils import run_bass_kernel_spmd as _run

    nc = _bacc.Bacc("TRN2", target_bir_lowering=False, num_devices=1)
    arrays, args = {}, []
    for name in _INS:
        a = _np.ascontiguousarray(inputs[name])
        arrays[f"in_{name}_dram"] = a
        args.append(nc.dram_tensor(f"in_{name}_dram", a.shape, _mybir.dt.from_np(a.dtype), kind="ExternalInput").ap())
    for i, (shape, dtype) in enumerate(_OUTS):
        dt = _mybir.dt.from_np(_np.dtype(dtype))
        args.append(nc.dram_tensor(f"out_{i}_dram", shape, dt, kind="ExternalOutput").ap())
    gnn_gated_recurrent_kernel(nc, *args)
    r = _run(nc, [arrays], core_ids=[0])
    got = tuple(r.results[0][f"out_{i}_dram"] for i in range(len(_OUTS)))
    return got[0]
```

```python
import concourse.bass as bass
from concourse import mybir
from contextlib import ExitStack


def gnn_gated_recurrent_kernel(nc, x, src, dst, W_msg, b_msg, W_ih, W_hh, b_ih, b_hh, out):
    f32, f16, i32 = mybir.dt.float32, mybir.dt.float16, mybir.dt.int32
    ALU, ACT, AX = mybir.AluOpType, mybir.ActivationFunctionType, mybir.AxisListType

    N, H = x.shape
    E = src.shape[0]
    STEPS = 5
    P = 128
    NCH = (N + P - 1) // P
    LASTP = N - (NCH - 1) * P
    TW = 512
    NT = (N + TW - 1) // TW
    TQ = TW // P
    RS = N + 1
    WIDTH = [min(TW, N - TW * j) for j in range(NT)]
    CHUNKS = [[(k, min(P, N - P * k)) for k in range(TQ * j, min(TQ * j + TQ, NCH))] for j in range(NT)]

    BLK = 5
    NB = N // BLK
    RH = 25
    RL = N // RH
    SW, LW = 128, RL + 1
    CAP = 256
    NS = CAP // P
    BG = 125
    NG = NB // BG
    SEG = 256
    NSMP = E // SEG
    BATCH = 4
    GRP = 25
    NGRP = NB // GRP
    SIZES = [BATCH] * (GRP // BATCH) + [GRP % BATCH]
    BPG = len(SIZES)
    SLOT = [b % 4 for b in range(BPG)]
    PRIOR = [3, 3, 3, 7, 4, 4, 4]
    HI_AFTER = [2 * j + 1 for j in range(NT)]
    assert TQ == 4 and HI_AFTER[-1] < 2 * BPG and 4 * BPG >= NCH
    LATE = 3
    LAG = LATE + 1
    EARLY = 4
    DIV_MUL, DIV_SHIFT = 4195, 19
    assert N == NB * BLK == RH * RL and NB == NG * BG and BLK * RH == 125
    assert all((r * DIV_MUL) >> DIV_SHIFT == r // RL for r in range(N)) and N * DIV_MUL < 2 ** 24

    ET = E // 125
    UN = 3
    assert NGRP % 2 == 1 and (NCH - LATE) % 2 == 0
    assert ET * 125 == E and ET % UN == 0 and STEPS % 2 == 1

    adj_dram = nc.dram_tensor("adj_scratch", [N, N], f16).ap()
    counts_dram = adj_dram.rearrange("(b c) (h l) -> (c h) b l", c=BLK, l=RL)
    msg_dram = nc.dram_tensor("msg_scratch", [N, H], f32).ap()

    with ExitStack() as ctx:
        def sb(name, shape, dt):
            return ctx.enter_context(nc.sbuf_tensor(name, shape, dt))

        def sem(name):
            return ctx.enter_context(nc.semaphore(name))

        adj = sb("adj", [P, NCH * RS], f16)
        hT = sb("hT", [P, RS], f32)
        msgs = sb("msgs", [P, 2 * NCH * 2 * H], f16)
        work = sb("work", [P, 5, TW], f32)
        aggT, rS, zS, nS, tS = (work[:, i, :] for i in range(5))
        WmT = sb("WmT", [P, H], f32)
        WihT = sb("WihT", [P, 3, H], f32)
        WhhT = sb("WhhT", [P, 3, H], f32)
        ident = sb("ident", [P, P], f32)
        iota = sb("iota", [P, P], f16)
        ones = sb("ones", [1, P], f32)
        ones2 = sb("ones2", [2, P], f16)
        bm2 = sb("bm2", [2, H], f16)
        bhi16 = sb("bhi16", [P, 1], f16)
        bhl = sb("bhl", [P, 2], f32)
        bcol = sb("bcol", [P, 8], f32)
        brz = sb("brz", [P, 2], f32)
        bnd = sb("bnd", [P, 4], f32)
        bndi = bnd[:, :].bitcast(i32)
        flag = sb("flag", [1, 1], i32)
        g_idx = sb("g_idx", [P, 1], i32)
        small = sb("small", [P, 50], f32)
        invs = bnd[:, 3:4]

        early = adj[:, :].bitcast(f32)
        take = [0]

        def carve(n, dt=f32):
            a = early[:, take[0]:take[0] + n]
            take[0] += n
            return a if dt is f32 else a.bitcast(dt)

        xs = carve(NCH * H).rearrange("p (k f) -> p k f", f=H)
        wnat = carve(7 * H).rearrange("p (k f) -> p k f", f=H)
        bnst = carve(NCH * 6).rearrange("p (k s) -> p k s", s=6)
        bnmv = carve(NCH * 2).rearrange("p (k s) -> p k s", s=2)
        lnve, lnsd, lnrs, lnnm = (carve(NCH) for _ in range(4))
        smp_i = carve(NSMP, i32)
        smp_f = carve(NSMP)
        junk = carve(SEG * 2)
        seg_i = carve(NG * SEG, i32).rearrange("p (g e) -> p g e", g=NG)
        seg_f = carve(NG * SEG).rearrange("p (g e) -> p g e", g=NG)
        dst_i = carve(NG * CAP, i32).rearrange("p (g e) -> p g e", g=NG)
        src_i = carve(NG * CAP, i32).rearrange("p (g e) -> p g e", g=NG)
        cl_f = carve(NG * CAP).rearrange("p (g e) -> p g e", g=NG)
        rm_i = carve(NG * CAP, i32).rearrange("p (g e) -> p g e", g=NG)
        rh_i = carve(NG * CAP, i32).rearrange("p (g e) -> p g e", g=NG)
        sk_f = carve(NG * CAP).rearrange("p (g e) -> p g e", g=NG)
        sc_f = carve(NG * CAP).rearrange("p (g e) -> p g e", g=NG)
        lk_f = carve(NG * CAP).rearrange("p (g e) -> p g e", g=NG)
        blk_i = carve(NG, i32)
        off_i = carve(NG, i32)
        start_i = carve(NG, i32)
        blk_f, cnt_a, off_f, cnt_b, start_f = (small[:, 5 * i:5 * i + 5] for i in range(5))
        nlow, nhigh, ndiff, onecol, nval = (small[:, 25 + 5 * i:30 + 5 * i] for i in range(5))
        assert take[0] < (NCH - LATE) * RS // 2

        keys = work[:, :, :].rearrange("p a b -> p (a b)").bitcast(f16)
        skey = keys[:, 0:NB * NS * 2]
        lkey = keys[:, NB * NS * 2:2 * NB * NS * 2]
        OHN = BATCH * NS
        oh_mem = [adj[:, (NCH - LATE) * RS + i * OHN * (SW + LW):] for i in range(4)]
        ohS = [m[:, 0:OHN * SW].rearrange("p (t j) -> p t j", t=OHN) for m in oh_mem]
        ohL = [m[:, OHN * SW:OHN * (SW + LW)].rearrange("p (t j) -> p t j", t=OHN) for m in oh_mem]
        assert 4 * OHN * (SW + LW) <= LATE * RS and 2 * GRP * RL <= NCH * 2 * H
        stage = msgs[:, NCH * 2 * H:NCH * 2 * H + 2 * GRP * RL]

        g_iota = early[:, 0:N]
        g_one = early[:, N:2 * N]
        g_dst = early[:, 2 * N:2 * N + ET].bitcast(i32)
        g_srci = early[:, 2 * N + ET:2 * N + 2 * ET].bitcast(i32)
        g_src = early[:, 2 * N + 2 * ET:2 * N + 3 * ET]
        g_msg = early[:, 7 * ET + 2 * N:7 * ET + 2 * N + H]
        g_agg = early[:, 8 * ET + 2 * N:8 * ET + 3 * N]
        g_node = early[:, 8 * ET + 3 * N:8 * ET + 3 * N + NCH * H]

        ps = ctx.enter_context(nc.psum_tensor("ps", [P, 8, TW], f32))
        psAgg = [ps[:, 0, :], ps[:, 1, :]]
        psR, psZ, psI, psH, psM = (ps[:, i, :] for i in range(2, 7))
        psX = ps[:, 7, :]
        blkps = [ps[:, 2 + i, :].rearrange("p (b j) -> p b j", j=P) for i in range(4)]
        FIRST = [EARLY] + list(range(EARLY)) + list(range(EARLY + 1, NT))
        acc0 = {j: ps[:, bank, :] for j, bank in enumerate((0, 1, 7, 6, 3, 0, 1))}
        assert EARLY == 4 and NT == 7
        next_bank = (7, 6, 7, 6, 7)
        init_bank = [(0, 1, 6)[j % 3] for j in range(NT)]
        g_psA = [ps[:, i, :] for i in range(NT)]

        consts = sem("consts")
        x_padded = sem("x_padded")
        x_loaded = sem("x_loaded")
        w_loaded = sem("w_loaded")
        b_loaded = sem("b_loaded")
        smp_loaded = sem("smp_loaded")
        smp_conv = sem("smp_conv")
        smp_spread = sem("smp_spread")
        coarse_off = sem("coarse_off")
        seg_loaded = sem("seg_loaded")
        fine_off = sem("fine_off")
        win_loaded = [sem(f"win_loaded{g}") for g in range(NG)]
        dv = sem("dv")
        ln_var = sem("ln_var")
        ln_sd = sem("ln_sd")
        ln_scale = sem("ln_scale")
        x_normed = sem("x_normed")
        xT_ready = sem("xT_ready")
        h0_ready = sem("h0_ready")
        wT_ready = sem("wT_ready")
        wT_copied = sem("wT_copied")
        wm_scaled = sem("wm_scaled")
        b_split = sem("b_split")
        dv_msg_pad = sem("dv_msg_pad")
        keys_ready = sem("keys_ready")
        keyT_ready = sem("keyT_ready")
        skey_copied = sem("skey_copied")
        lkey_copied = sem("lkey_copied")
        chunk_summed = sem("chunk_summed")
        msgs_moved = sem("msgs_moved")
        nval_ready = sem("nval_ready")
        nval_summed = sem("nval_summed")
        flag_ready = sem("flag_ready")
        onehots_ready = sem("onehots_ready")
        blocks_done = sem("blocks_done")
        counts_staged = sem("counts_staged")
        stage_written = [sem("stage_written_even"), sem("stage_written_odd")]
        adj_loaded = sem("adj_loaded")
        late_loaded = [sem(f"late_loaded{i}") for i in range(LATE)]
        last_cleared = sem("last_cleared")
        agg_done = sem("agg_done")
        aggT_ready = sem("aggT_ready")
        r_summed = sem("r_summed")
        z_summed = sem("z_summed")
        n_summed = sem("n_summed")
        r_ready = sem("r_ready")
        z_ready = sem("z_ready")
        gated = sem("gated")
        n_arg = sem("n_arg")
        n_ready = sem("n_ready")
        h_minus_n = sem("h_minus_n")
        z_times = sem("z_times")
        h_ready = sem("h_ready")
        msg_done = sem("msg_done")
        msg_hi = sem("msg_hi")
        msg_lo = sem("msg_lo")
        x_again = sem("x_again")
        outT_done = sem("outT_done")
        out_added = sem("out_added")
        out_written = sem("out_written")
        g_consts = sem("g_consts")
        g_edges = sem("g_edges")
        g_conv = sem("g_conv")
        g_index = sem("g_index")
        g_node_ready = sem("g_node_ready")
        g_node_sum = sem("g_node_sum")
        g_node_written = sem("g_node_written")
        g_gathered = [sem(f"g_gathered{i}") for i in range(UN)]
        g_onehot = sem("g_onehot")
        g_tile_done = sem("g_tile_done")
        g_copied = sem("g_copied")
        pool_turn = sem("pool_turn")
        sp_turn = sem("sp_turn")
        block = ctx.enter_context(nc.Block())

        def past(n):
            return n + 1

        def mpart(par, k, part):
            return par * (NCH * 2 * H) + (k * 2 + part) * H

        @block.sync
        def _(sp):
            ctx.enter_context(nc.allow_non_contiguous_dma(reason="samples and bias columns: a few hundred single elements"))
            sp.dma_start(smp_i[0:1, :], dst[0:NSMP * SEG].rearrange("(a n s) -> a n s", a=1, s=SEG)[:, :, SEG - 1]
                         ).then_inc(smp_loaded, 16)
            sp.dma_start(xs[:, 0:NCH - 1, :], x[0:(NCH - 1) * P, :].rearrange("(k p) f -> p k f", p=P)
                         ).then_inc(x_loaded, 16)
            sp.wait_ge(x_padded, 1)
            sp.dma_start(xs[0:LASTP, NCH - 1, :], x[(NCH - 1) * P:N, :]).then_inc(x_loaded, 16)
            sp.dma_start(wnat[:, 0, :], W_msg).then_inc(w_loaded, 16)
            sp.dma_start(wnat[:, 1:4, :], W_ih.rearrange("(g p) f -> p g f", p=P)).then_inc(w_loaded, 16)
            sp.dma_start(wnat[:, 4:7, :], W_hh.rearrange("(g p) f -> p g f", p=P)).then_inc(w_loaded, 16)
            sp.dma_start(bcol[:, 0:3], b_ih.rearrange("(g p) -> p g", p=P)).then_inc(b_loaded, 16)
            sp.dma_start(bcol[:, 3:6], b_hh.rearrange("(g p) -> p g", p=P)).then_inc(b_loaded, 16)
            sp.dma_start(bcol[:, 6:7], b_msg.rearrange("(p a) -> p a", a=1)).then_inc(b_loaded, 16)
            def write_counts(g, par):
                sp.wait_ge(counts_staged, BPG * (g + 1))
                sp.sem_inc(sp_turn, 1)
                slot = stage[:, par * GRP * RL:(par + 1) * GRP * RL].rearrange("p (b j) -> p b j", j=RL)
                to = counts_dram[:, bass.ds(g * GRP, GRP), :]
                sp.dma_start(to[0:120], slot[0:120]).then_inc(stage_written[par], 16)
                sp.dma_start(to[120:125], slot[120:125]).then_inc(stage_written[par], 16)

            write_counts(0, 0)
            with sp.Fori(1, NGRP - 1, 2) as g:
                write_counts(g, 1)
                write_counts(g + 1, 0)
            sp.wait_ge(flag_ready, 1)
            fast = sp.value_load(flag[0:1, 0:1], min_val=0, max_val=1)
            with sp.If(fast):
                sp.wait_ge(msgs_moved, STEPS - 1)
                xres = msgs[:, mpart(1, 0, 0):].bitcast(f32).rearrange("p (k f) -> p k f", f=H)
                sp.dma_start(xres[:, 0:NCH - 1, :], x[0:(NCH - 1) * P, :].rearrange("(k p) f -> p k f", p=P)
                             ).then_inc(x_again, 16)
                sp.dma_start(xres[0:LASTP, NCH - 1, :], x[(NCH - 1) * P:N, :]).then_inc(x_again, 16)
                for j in range(NT):
                    sp.wait_ge(out_added, j + 1)
                    k0, n = CHUNKS[j][0][0], len(CHUNKS[j])
                    if WIDTH[j] == TW:
                        sp.dma_start(out[TW * j:TW * (j + 1), :].rearrange("(k p) f -> p k f", p=P),
                                     xres[:, k0:k0 + n, :]).then_inc(out_written, 16)
                    else:
                        sp.dma_start(out[TW * j:N, :], xres[0:LASTP, k0, :]).then_inc(out_written, 16)
                sp.wait_ge(out_written, 16 * NT)
            with sp.Else():
                sp.wait_ge(chunk_summed, NCH - LATE)
                sp.wait_ge(stage_written[0], 32 * (NGRP // 2 + 1))
                sp.wait_ge(stage_written[1], 32 * (NGRP // 2))
                sp.dma_start(g_dst[0:125, :], dst.rearrange("(p t) -> p t", t=ET)).then_inc(g_edges, 16)
                sp.dma_start(g_srci[0:125, :], src.rearrange("(p t) -> p t", t=ET)).then_inc(g_edges, 16)
                node = g_node.rearrange("p (k f) -> p k f", f=H)
                with sp.Fori(0, STEPS) as s:
                    sp.wait_ge(g_node_ready, past(NT * (s + 1)))
                    sp.sem_inc(sp_turn, 1)
                    sp.dma_start(msg_dram[0:(NCH - 1) * P, :].rearrange("(k p) f -> p k f", p=P),
                                 node[:, 0:NCH - 1, :]).then_inc(g_node_written, 16)
                    sp.dma_start(msg_dram[(NCH - 1) * P:N, :], node[0:LASTP, NCH - 1, :]).then_inc(g_node_written, 16)
                sp.wait_ge(agg_done, past(STEPS * NT))
                sp.wait_ge(h_ready, past(STEPS * NT))
                sp.dma_start(node[:, 0:NCH - 1, :], x[0:(NCH - 1) * P, :].rearrange("(k p) f -> p k f", p=P)
                             ).then_inc(x_again, 16)
                sp.dma_start(node[0:LASTP, NCH - 1, :], x[(NCH - 1) * P:N, :]).then_inc(x_again, 16)
                sp.wait_ge(out_added, NT)
                sp.dma_start(out[0:(NCH - 1) * P, :].rearrange("(k p) f -> p k f", p=P),
                             node[:, 0:NCH - 1, :]).then_inc(out_written, 16)
                sp.dma_start(out[(NCH - 1) * P:N, :], node[0:LASTP, NCH - 1, :]).then_inc(out_written, 16)
                sp.wait_ge(out_written, 32)

        @block.gpsimd
        def _(pool):
            pool.iota(blk_i[0:BG, :], pattern=[[BLK * BG, NG]], base=0, channel_multiplier=BLK).then_inc(consts, 1)
            pool.memset(ident[:, :], 0.0).then_inc(consts, 1)
            pool.memset(ones[:, :], 1.0).then_inc(consts, 1)
            pool.memset(ones2[:, :], 1.0).then_inc(consts, 1)
            pool.wait_ge(consts, 4)
            pool.affine_select(out=ident[:, :], in_=ident[:, :], compare_op=ALU.not_equal, fill=1.0, base=0,
                               pattern=[[-1, P]], channel_multiplier=1).then_inc(consts, 1)
            pool.iota(iota[:, :], pattern=[[1, P]], base=0, channel_multiplier=0,
                      allow_small_or_imprecise_dtypes=True).then_inc(consts, 1)
            flat = [a.rearrange("(a b) -> a b", a=1) for a in (dst, src)]

            def gather(to, g, offsets, of, done):
                pool.indirect_dma_start(out=to[0:BG, g, :], out_offset=None, in_=flat[of],
                                        in_offset=bass.IndirectOffsetOnAxis(ap=offsets[0:BG, g:g + 1], axis=1)
                                        ).then_inc(done, 16)

            pool.wait_ge(coarse_off, 1)
            for g in range(NG):
                gather(seg_i, g, off_i, 0, seg_loaded)
            pool.wait_ge(fine_off, 1)
            for g in range(NG):
                gather(dst_i, g, start_i, 0, win_loaded[g])
                gather(src_i, g, start_i, 1, win_loaded[g])

            def groups_written(k, par):
                pool.wait_ge(stage_written[0], 16 * k + 32 + 16 * par)
                pool.wait_ge(stage_written[1], 16 * k + 32 - 16 * par)

            def load_chunk(k, par, rows, first=False):
                groups_written(k, par)
                if not first:
                    pool.wait_ge(adj_loaded, 16 * k)
                pool.dma_start(adj[0:rows, bass.ds(k * RS, N)], adj_dram[bass.ds(k * P, rows), :]
                               ).then_inc(adj_loaded, 16)

            pool.wait_ge(keyT_ready, NG)
            pool.wait_ge(nval_ready, 1)
            load_chunk(0, 0, P, first=True)
            with pool.Fori(1, NCH - LATE - 1, 2) as k:
                load_chunk(k, 1, P)
                load_chunk(k + 1, 0, P)
            load_chunk(NCH - LATE - 1, 1, P)
            pool.wait_ge(flag_ready, 1)
            fast = pool.value_load(flag[0:1, 0:1], min_val=0, max_val=1)
            with pool.If(fast):
                pool.wait_ge(last_cleared, 1)
                for k in range(NCH - LATE, NCH):
                    rows = min(P, N - k * P)
                    groups_written(min(k, NGRP - 2), min(k, NGRP - 2) % 2)
                    pool.dma_start(adj[0:rows, k * RS:k * RS + N], adj_dram[k * P:k * P + rows, :]
                                   ).then_inc(late_loaded[k - NCH], 16)
            with pool.Else():
                pool.wait_ge(chunk_summed, NCH - LATE)
                pool.iota(g_iota, pattern=[[1, N]], base=0, channel_multiplier=0,
                          allow_small_or_imprecise_dtypes=True).then_inc(g_consts, 1)
                pool.wait_ge(g_edges, 32)
                with pool.Fori(0, STEPS) as s:
                    pool.wait_ge(g_node_written, 32 * (s + 1))
                    pool.sem_inc(pool_turn, 1)
                    with pool.Fori(0, ET // UN) as u:
                        for i in range(UN):
                            pool.wait_ge(g_index, s * ET + u * UN + (i + 1))
                            pool.sem_inc(pool_turn, 1)
                            pool.indirect_dma_start(
                                out=g_msg[0:125, :], out_offset=None, in_=msg_dram,
                                in_offset=bass.IndirectOffsetOnAxis(ap=g_idx[0:125, :], axis=0)
                            ).then_inc(g_gathered[i], 16)

        @block.vector
        def _(v):
            for started in (n_arg, h_ready, g_node_ready):
                v.sem_inc(started, 1)
            chain = [0]

            def link(ins):
                chain[0] += 1
                ins.then_inc(dv, 1)
                v.wait_ge(dv, chain[0])

            nc.vector.memset(xs[0:P, NCH - 1, :], 0.0).then_inc(x_padded, 1)
            link(nc.vector.memset(small[:, :], 0.0))
            link(nc.vector.memset(onecol[:, :], 1.0))
            v.wait_ge(smp_loaded, 16)
            nc.vector.tensor_copy(smp_f[0:1, :], smp_i[0:1, :]).then_inc(smp_conv, 1)
            v.wait_ge(consts, 6)
            link(nc.vector.tensor_copy(blk_f[0:BG, :], blk_i[0:BG, :]))
            v.wait_ge(smp_spread, 1)
            for g in range(NG):
                link(nc.vector.tensor_scalar(junk[0:BG, 0:NSMP], psX[0:BG, 0:NSMP], blk_f[0:BG, g:g + 1], None,
                                             ALU.is_lt, op1=ALU.add, accum_out=cnt_a[0:BG, g:g + 1]))
            link(nc.vector.tensor_scalar(off_f[0:BG, :], cnt_a[0:BG, :], float(SEG), float(E - SEG), ALU.mult, ALU.min))
            nc.vector.tensor_copy(off_i[0:BG, :], off_f[0:BG, :]).then_inc(coarse_off, 1)
            v.wait_ge(x_loaded, 32)
            for k in range(NCH):
                nc.vector.bn_stats(bnst[:, k, :], xs[:, k, :]).then_inc(dv, 1)
            chain[0] += NCH
            v.wait_ge(dv, chain[0])
            for k in range(NCH):
                nc.vector.bn_aggr(bnmv[:, k, :], bnst[:, k, :]).then_inc(dv, 1)
            chain[0] += NCH
            v.wait_ge(dv, chain[0])
            nc.vector.tensor_scalar(lnve, bnmv[:, :, 1], 1e-5, None, ALU.add).then_inc(ln_var, 1)
            v.wait_ge(seg_loaded, 16 * NG)
            link(nc.vector.tensor_copy(seg_f[0:BG], seg_i[0:BG]))
            for g in range(NG):
                link(nc.vector.tensor_scalar(junk[0:BG, 0:SEG], seg_f[0:BG, g, :], blk_f[0:BG, g:g + 1], None,
                                             ALU.is_lt, op1=ALU.add, accum_out=cnt_b[0:BG, g:g + 1]))
            link(nc.vector.tensor_tensor(start_f[0:BG, :], off_f[0:BG, :], cnt_b[0:BG, :], ALU.add))
            nc.vector.tensor_scalar(start_i[0:BG, :], start_f[0:BG, :], float(E - CAP), None, ALU.min
                                    ).then_inc(fine_off, 1)
            v.wait_ge(ln_sd, 1)
            link(nc.vector.reciprocal(lnrs, lnsd))
            nc.vector.scalar_tensor_tensor(out=lnnm, in0=bnmv[:, :, 0], scalar=-1.0, in1=lnrs,
                                           op0=ALU.mult, op1=ALU.mult).then_inc(ln_scale, 1)
            v.wait_ge(w_loaded, 48)
            v.wait_ge(b_loaded, 48)
            link(nc.vector.tensor_reduce(bnd[:, 0:1], wnat[:, 0, :], AX.X, ALU.add, apply_absolute_value=True))
            link(nc.vector.tensor_scalar(bcol[:, 7:8].bitcast(i32), bcol[:, 6:7].bitcast(i32), 0x7FFFFFFF, None,
                                         ALU.bitwise_and))
            link(nc.vector.tensor_scalar(bnd[:, 1:2], bnd[:, 0:1], 12.0, 1e-30, ALU.mult, ALU.add))
            link(nc.vector.tensor_tensor(bnd[:, 0:1], bnd[:, 1:2], bcol[:, 7:8], ALU.add))
            link(nc.vector.tensor_scalar(bndi[:, 1:2], bndi[:, 0:1], 0x7F800000, None, ALU.bitwise_and))
            link(nc.vector.tensor_scalar(bndi[:, 2:3], bndi[:, 1:2], 0x7F800000, None, ALU.bitwise_xor))
            link(nc.vector.tensor_scalar(bnd[:, 2:3], bnd[:, 2:3], float(2 ** 13), None, ALU.mult))
            nc.vector.tensor_scalar(wnat[:, 0, :], wnat[:, 0, :], bnd[:, 2:3], None, ALU.mult).then_inc(wm_scaled, 1)
            link(nc.vector.tensor_scalar(bnd[:, 3:4], bnd[:, 1:2], float(2 ** -14), None, ALU.mult))
            link(nc.vector.tensor_tensor(brz[:, :], bcol[:, 0:2], bcol[:, 3:5], ALU.add))
            link(nc.vector.tensor_scalar(bcol[:, 7:8], bcol[:, 6:7], bnd[:, 2:3], None, ALU.mult))
            link(nc.vector.tensor_copy(bhi16[:, :], bcol[:, 7:8]))
            link(nc.vector.tensor_copy(bhl[:, 0:1], bhi16[:, :]))
            nc.vector.tensor_tensor(bhl[:, 1:2], bcol[:, 7:8], bhi16[:, :], ALU.subtract).then_inc(b_split, 1)
            nc.vector.memset(msgs[:, mpart(0, NCH - 1, 0):mpart(0, NCH - 1, 2)], 0.0).then_inc(dv_msg_pad, 1)

            def lo_part(m, par, j, bank=6):
                v.wait_ge(msg_hi, m + 1)
                rows, n, k0 = CHUNKS[j][-1][1], len(CHUNKS[j]), CHUNKS[j][0][0]
                tile = msgs[0:rows, mpart(par, k0, 0):mpart(par, k0 + n, 0)].rearrange("p (k a f) -> p k a f", a=2, f=H)
                nc.vector.tensor_tensor(tile[:, :, 1, :], ps[0:rows, bank, 0:n * H].rearrange("p (k f) -> p k f", f=H),
                                        tile[:, :, 0, :], ALU.subtract).then_inc(msg_lo, 1)

            def edge_keys(g):
                v.wait_ge(win_loaded[g], 32)
                nc.vector.tensor_scalar(rm_i[0:BG, g], src_i[0:BG, g], float(DIV_MUL), None, ALU.mult).then_inc(dv, 1)
                nc.vector.tensor_scalar(cl_f[0:BG, g], dst_i[0:BG, g], blk_f[0:BG, g:g + 1], None, ALU.subtract
                                        ).then_inc(dv, 1)
                chain[0] += 2
                v.wait_ge(dv, chain[0])
                link(nc.vector.tensor_scalar(rh_i[0:BG, g], rm_i[0:BG, g], DIV_SHIFT, None, ALU.logical_shift_right))
                link(nc.vector.scalar_tensor_tensor(out=sk_f[0:BG, g], in0=cl_f[0:BG, g], scalar=float(RH),
                                                    in1=rh_i[0:BG, g], op0=ALU.mult, op1=ALU.add))
                link(nc.vector.tensor_scalar(sc_f[0:BG, g], sk_f[0:BG, g], -1.0, 255.0, ALU.max, ALU.min))
                nc.vector.scalar_tensor_tensor(out=lk_f[0:BG, g], in0=rh_i[0:BG, g], scalar=float(-RL),
                                               in1=src_i[0:BG, g], op0=ALU.mult, op1=ALU.add).then_inc(keys_ready, 1)
                nc.vector.tensor_scalar(seg_f[0:BG, g], cl_f[0:BG, g], float(BLK), None, ALU.is_lt, op1=ALU.add,
                                        accum_out=nlow[0:BG, g:g + 1]).then_inc(dv, 1)
                nc.vector.tensor_scalar(junk[0:BG, 0:CAP], cl_f[0:BG, g], 0.0, None, ALU.is_lt, op1=ALU.add,
                                        accum_out=nhigh[0:BG, g:g + 1]).then_inc(dv, 1)
                chain[0] += 2

            def copy_skey(g):
                v.wait_ge(keyT_ready, g + 1)
                nc.vector.tensor_copy(
                    skey.rearrange("p (b s d) -> p b s d", s=NS, d=2)[:, BG * g:BG * (g + 1)],
                    ps[:, 4, 0:NS * P].rearrange("p (s b d) -> p b s d", s=NS, d=1)[:, 0:BG]
                    .broadcast_to([P, BG, NS, 2])).then_inc(skey_copied, 1)

            for g in range(NG):
                edge_keys(g)
                if g >= 1:
                    copy_skey(g - 1)
            copy_skey(NG - 1)
            v.wait_ge(dv, chain[0])
            link(nc.vector.tensor_tensor(ndiff[:, :], nlow[:, :], nhigh[:, :], ALU.subtract))
            nc.vector.tensor_reduce(nval[:, 0:1], ndiff[:, :], AX.X, ALU.add).then_inc(nval_ready, 1)

            def onehots(b, kcol, prior):
                if prior is not None:
                    v.wait_ge(blocks_done, prior)
                n = SIZES[b] * NS
                for oh, key, w in ((ohS, skey, SW), (ohL, lkey, LW)):
                    k4 = key[:, bass.ds(kcol, n * 2)].rearrange("p (t o d) -> p t o d", o=1, d=2)
                    i4 = iota[:, 0:w].rearrange("p (o j d) -> p o j d", o=1, d=2)
                    shape = [P, n, w // 2, 2]
                    nc.vector.tensor_tensor(oh[SLOT[b]][:, 0:n].rearrange("p t (j d) -> p t j d", d=2),
                                            k4.broadcast_to(shape), i4.broadcast_to(shape), ALU.is_equal
                                            ).then_inc(onehots_ready, 1)

            v.wait_ge(lkey_copied, NG)
            def lo_after(i):
                if i - 2 in HI_AFTER:
                    j = HI_AFTER.index(i - 2)
                    lo_part(j, 0, j, init_bank[j])

            for b in range(BPG):
                onehots(b, b * OHN * 2, b - 3 if b >= 4 else None)
                lo_after(b)
            for b in range(BPG):
                onehots(b, GRP * NS * 2 + b * OHN * 2, BPG + b - PRIOR[b] + 1)
                lo_after(BPG + b)
            lo_after(2 * BPG + 1)
            v.wait_ge(nval_summed, 1)
            nc.vector.tensor_scalar(flag[0:1, 0:1], psX[0:1, 0:1], float(E), None, ALU.is_equal).then_inc(flag_ready, 1)
            with v.Fori(2, NGRP) as g:
                for b in range(BPG):
                    onehots(b, g * (GRP * NS * 2) + b * OHN * 2, g * BPG + (b - PRIOR[b] + 1))
            v.wait_ge(flag_ready, 1)
            fast = v.value_load(flag[0:1, 0:1], min_val=0, max_val=1)

            def gates(g, cols, w):
                v.wait_ge(r_ready, past(g + 1))
                v.wait_ge(n_summed, g + 1)
                v.wait_ge(n_ready, past(g))
                nc.vector.scalar_tensor_tensor(out=tS[:, 0:w], in0=psH[:, 0:w], scalar=bcol[:, 5:6], in1=rS[:, 0:w],
                                               op0=ALU.add, op1=ALU.mult).then_inc(gated, 1)
                v.wait_ge(gated, g + 1)
                nc.vector.tensor_tensor(tS[:, 0:w], psI[:, 0:w], tS[:, 0:w], ALU.add).then_inc(n_arg, 1)
                v.wait_ge(n_ready, past(g + 1))
                h = hT[:, cols:cols + w]
                nc.vector.tensor_tensor(rS[:, 0:w], h, nS[:, 0:w], ALU.subtract).then_inc(h_minus_n, 1)
                v.wait_ge(h_minus_n, g + 1)
                v.wait_ge(z_ready, past(g + 1))
                nc.vector.tensor_tensor(rS[:, 0:w], rS[:, 0:w], zS[:, 0:w], ALU.mult).then_inc(z_times, 1)
                v.wait_ge(z_times, g + 1)
                nc.vector.tensor_tensor(h, rS[:, 0:w], nS[:, 0:w], ALU.add).then_inc(h_ready, 1)

            with v.If(fast):
                v.wait_ge(blocks_done, NGRP * BPG)
                nc.vector.memset(adj[:, (NCH - 1) * RS:NCH * RS], 0.0).then_inc(last_cleared, 1)
                v.wait_ge(stage_written[0], 32 * (NGRP // 2 + 1))
                v.wait_ge(stage_written[1], 32 * (NGRP // 2))

                def move_messages(s):
                    v.wait_ge(agg_done, past(NT * (s + 1)))
                    v.wait_ge(msg_lo, NT * (s + 1) + EARLY)
                    nc.vector.tensor_copy(msgs[:, mpart(0, 0, 0):mpart(0, TQ * EARLY, 0)],
                                          msgs[:, mpart(1, 0, 0):mpart(1, TQ * EARLY, 0)]).then_inc(msgs_moved, 1)

                def first_step():
                    for g in range(EARLY + 1):
                        gates(g, TW * FIRST[g], TW)
                        if g == EARLY - 1:
                            lo_part(NT, 1, 0, next_bank[0])
                    for j in range(1, EARLY):
                        lo_part(NT + j, 1, j, next_bank[j])
                    move_messages(0)
                    gates(NT - 2, TW * (NT - 2), TW)
                    lo_part(NT + EARLY, 0, EARLY, next_bank[EARLY])
                    gates(NT - 1, TW * (NT - 1), WIDTH[NT - 1])

                def step(s, last):
                    g0 = s * NT
                    lo_part(g0 + NT - 2, 0, NT - 2)
                    lo_part(g0 + NT - 1, 0, NT - 1)
                    for j in range(NT):
                        gates(g0 + j, TW * j, WIDTH[j])
                        if last:
                            if j >= 1:
                                add_x(j - 1)
                        elif 1 <= j <= EARLY:
                            lo_part(g0 + NT + j - 1, 1, j - 1)
                            if j == EARLY:
                                move_messages(s)
                        elif j == NT - 2:
                            lo_part(g0 + NT + j - 1, 0, j - 1)
                    if last:
                        add_x(NT - 1)

                xres = msgs[:, mpart(1, 0, 0):].bitcast(f32).rearrange("p (k f) -> p k f", f=H)

                def add_x(j):
                    v.wait_ge(outT_done, j + 1)
                    if j == 0:
                        v.wait_ge(x_again, 32)
                    rows, n, k0 = CHUNKS[j][-1][1], len(CHUNKS[j]), CHUNKS[j][0][0]
                    nc.vector.tensor_tensor(xres[0:rows, k0:k0 + n, :],
                                            psM[0:rows, 0:n * H].rearrange("p (k f) -> p k f", f=H),
                                            xres[0:rows, k0:k0 + n, :], ALU.add).then_inc(out_added, 1)

                first_step()
                with v.Fori(1, STEPS - 1) as s:
                    step(s, False)
                step(STEPS - 1, True)
            with v.Else():
                v.wait_ge(g_edges, 32)
                nc.vector.tensor_copy(g_src[0:125, :], g_srci[0:125, :]).then_inc(g_conv, 1)
                v.wait_ge(g_conv, 1)
                v.wait_ge(g_consts, 1)
                node = g_node.rearrange("p (k f) -> p k f", f=H)
                with v.Fori(0, STEPS) as s:
                    for j in range(NT):
                        rows, n, k0 = CHUNKS[j][-1][1], len(CHUNKS[j]), CHUNKS[j][0][0]
                        v.wait_ge(g_node_sum, s * NT + j + 1)
                        v.wait_ge(agg_done, past(NT * s))
                        nc.vector.tensor_copy(node[0:rows, k0:k0 + n, :],
                                              psM[0:rows, 0:n * H].rearrange("p (k f) -> p k f", f=H)
                                              ).then_inc(g_node_ready, 1)
                    with v.Fori(0, ET) as t:
                        v.wait_ge(g_tile_done, past(s * ET + t))
                        nc.vector.tensor_copy(g_idx[0:125, :], g_dst[0:125, bass.ds(t, 1)]).then_inc(g_index, 1)
                        nc.vector.tensor_scalar(g_one[0:125, :], g_iota[0:125, :], g_src[0:125, bass.ds(t, 1)], None,
                                                ALU.is_equal).then_inc(g_onehot, 1)
                    v.wait_ge(agg_done, past(NT * (s + 1)))
                    for j in range(NT):
                        nc.vector.tensor_scalar(g_agg[:, TW * j:TW * j + WIDTH[j]], ps[:, j, 0:WIDTH[j]], invs, None,
                                                ALU.mult).then_inc(g_copied, 1)
                    for j in range(NT):
                        gates(s * NT + j, TW * j, WIDTH[j])
                v.wait_ge(x_again, 32)
                for j in range(NT):
                    rows, n, k0 = CHUNKS[j][-1][1], len(CHUNKS[j]), CHUNKS[j][0][0]
                    v.wait_ge(outT_done, j + 1)
                    nc.vector.tensor_tensor(node[0:rows, k0:k0 + n, :],
                                            psM[0:rows, 0:n * H].rearrange("p (k f) -> p k f", f=H),
                                            node[0:rows, k0:k0 + n, :], ALU.add).then_inc(out_added, 1)

        @block.scalar
        def _(act):
            for started in (r_ready, z_ready, n_ready, aggT_ready):
                act.sem_inc(started, 1)
            act.wait_ge(ln_var, 1)
            nc.scalar.activation(lnsd, lnve, ACT.Sqrt).then_inc(ln_sd, 1)
            act.wait_ge(ln_scale, 1)
            for k in range(NCH):
                nc.scalar.activation(xs[:, k, :], xs[:, k, :], ACT.Relu, bias=lnnm[:, k:k + 1],
                                     scale=lnrs[:, k:k + 1]).then_inc(x_normed, 1)
            act.wait_ge(wT_ready, 1)
            nc.scalar.activation(WmT[:, :], ps[:, 0, 0:P], ACT.Copy).then_inc(wT_copied, 1)
            nc.scalar.activation(WihT[:, :, :], ps[:, 0, P:4 * P].rearrange("p (g f) -> p g f", g=3), ACT.Copy
                                 ).then_inc(wT_copied, 1)
            nc.scalar.activation(WhhT[:, :, :], ps[:, 1, 0:3 * P].rearrange("p (g f) -> p g f", g=3), ACT.Copy
                                 ).then_inc(wT_copied, 1)
            nc.scalar.activation(bm2[:, :], ps[0:2, 1, 3 * P:4 * P], ACT.Copy).then_inc(wT_copied, 1)
            def hi_part(m, par, j, bank=6):
                act.wait_ge(msg_done, m + 1)
                rows, n, k0 = CHUNKS[j][-1][1], len(CHUNKS[j]), CHUNKS[j][0][0]
                tile = msgs[0:rows, mpart(par, k0, 0):mpart(par, k0 + n, 0)].rearrange("p (k a f) -> p k a f", a=2, f=H)
                nc.scalar.activation(tile[:, :, 0, :], ps[0:rows, bank, 0:n * H].rearrange("p (k f) -> p k f", f=H),
                                     ACT.Copy).then_inc(msg_hi, 1)

            def copy_lkey(g):
                act.wait_ge(keyT_ready, g + 1)
                nc.scalar.activation(
                    lkey.rearrange("p (b s d) -> p b s d", s=NS, d=2)[:, BG * g:BG * (g + 1)],
                    ps[:, 5, 0:NS * P].rearrange("p (s b d) -> p b s d", s=NS, d=1)[:, 0:BG]
                    .broadcast_to([P, BG, NS, 2]), ACT.Copy).then_inc(lkey_copied, 1)

            copy_lkey(0)
            copy_lkey(1)
            for j in range(NT):
                act.wait_ge(xT_ready, j + 1)
                nc.scalar.activation(hT[:, TW * j:TW * j + WIDTH[j]], ps[:, 2 + j % 2, 0:WIDTH[j]], ACT.Copy
                                     ).then_inc(h0_ready, 1)
            for g in range(2, NG):
                copy_lkey(g)
            act.wait_ge(dv_msg_pad, 1)

            def stage_batch(b, par, ready, free=None):
                act.wait_ge(blocks_done, ready)
                if b == 0 and free is not None:
                    act.wait_ge(stage_written[par], free)
                col = (par * GRP + b * BATCH) * RL
                nc.scalar.activation(stage[0:125, col:col + SIZES[b] * RL].rearrange("p (b j) -> p b j", j=RL),
                                     blkps[SLOT[b]][0:125, 0:SIZES[b], 0:RL], ACT.Copy).then_inc(counts_staged, 1)

            for g in range(2):
                for b in range(BPG):
                    stage_batch(b, g, g * BPG + b + 1)
                    if g * BPG + b in HI_AFTER:
                        j = HI_AFTER.index(g * BPG + b)
                        hi_part(j, 0, j, init_bank[j])
            for b in range(BPG):
                stage_batch(b, 0, 2 * BPG + b + 1, 32)
            with act.Fori(3, NGRP - 1, 2) as g:
                for b in range(BPG):
                    stage_batch(b, 1, g * BPG + b + 1, 16 * (g - 1))
                for b in range(BPG):
                    stage_batch(b, 0, g * BPG + BPG + b + 1, 16 * (g + 1))
            act.wait_ge(flag_ready, 1)
            fast = act.value_load(flag[0:1, 0:1], min_val=0, max_val=1)

            def gates(g, w):
                act.wait_ge(r_summed, g + 1)
                act.wait_ge(h_ready, past(g))
                nc.scalar.activation(rS[:, 0:w], psR[:, 0:w], ACT.Sigmoid, bias=brz[:, 0:1]).then_inc(r_ready, 1)
                act.wait_ge(z_summed, past(g + 1))
                nc.scalar.activation(zS[:, 0:w], psZ[:, 0:w], ACT.Sigmoid, bias=brz[:, 1:2]).then_inc(z_ready, 1)
                act.wait_ge(n_arg, past(g + 1))
                nc.scalar.activation(nS[:, 0:w], tS[:, 0:w], ACT.Tanh, bias=bcol[:, 2:3]).then_inc(n_ready, 1)

            with act.If(fast):
                def evac(g, w, bank):
                    act.wait_ge(agg_done, past(g + 1))
                    act.wait_ge(z_summed, past(g))
                    nc.scalar.activation(aggT[:, 0:w], bank[:, 0:w], ACT.Identity, scale=invs
                                         ).then_inc(aggT_ready, 1)

                act.wait_ge(stage_written[0], 32 * (NGRP // 2 + 1))
                act.wait_ge(stage_written[1], 32 * (NGRP // 2))

                def first_step():
                    evac(0, TW, acc0[FIRST[0]])
                    for g in range(EARLY + 1):
                        if g < EARLY:
                            evac(g + 1, TW, acc0[FIRST[g + 1]])
                        gates(g, TW)
                        if g == EARLY - 1:
                            hi_part(NT, 1, 0, next_bank[0])
                    evac(EARLY + 1, TW, acc0[FIRST[EARLY + 1]])
                    for j in range(1, EARLY):
                        hi_part(NT + j, 1, j, next_bank[j])
                    evac(NT - 1, WIDTH[NT - 1], acc0[NT - 1])
                    gates(NT - 2, TW)
                    hi_part(NT + EARLY, 0, EARLY, next_bank[EARLY])
                    gates(NT - 1, WIDTH[NT - 1])

                def step(s, last):
                    g0 = s * NT
                    hi_part(g0 + NT - 2, 0, NT - 2)
                    hi_part(g0 + NT - 1, 0, NT - 1)
                    evac(g0, TW, psAgg[0])
                    for j in range(NT):
                        if j < NT - 1:
                            evac(g0 + j + 1, WIDTH[j + 1], psAgg[(j + 1) % 2])
                        gates(g0 + j, WIDTH[j])
                        if not last and 1 <= j < NT - 1:
                            hi_part(g0 + NT + j - 1, 1 if j <= EARLY else 0, j - 1)

                first_step()
                with act.Fori(1, STEPS - 1) as s:
                    step(s, False)
                step(STEPS - 1, True)
            with act.Else():
                with act.Fori(0, STEPS) as s:
                    for j in range(NT):
                        gates(s * NT + j, WIDTH[j])

        @block.tensor
        def _(pe):
            for started in (z_summed, agg_done, g_tile_done):
                pe.sem_inc(started, 1)
            pe.wait_ge(smp_conv, 1)
            pe.wait_ge(consts, 6)
            nc.tensor.matmul(psX[0:BG, 0:NSMP], ones[0:1, 0:BG], smp_f[0:1, :], start=True, stop=True
                             ).then_inc(smp_spread, 1)
            pe.wait_ge(wm_scaled, 1)
            for i in range(7):
                nc.tensor.transpose(ps[:, i // 4, (i % 4) * P:(i % 4 + 1) * P], wnat[:, i, :], ident[:, :])
            pe.wait_ge(b_split, 1)
            nc.tensor.matmul(ps[0:2, 1, 3 * P:4 * P], bhl[:, :], ident[:, :], start=True, stop=True
                             ).then_inc(wT_ready, 1)
            def node_product(chunks, bank=6):
                for k, rows in chunks:
                    to = ps[0:rows, bank, (k % TQ) * H:(k % TQ + 1) * H]
                    nc.tensor.matmul(to, hT[:, P * k:P * k + rows], WmT[:, :], start=True, stop=False)
                    last = nc.tensor.matmul(to, ones2[0:2, 0:rows], bm2[0:2, :], start=False, stop=True)
                return last

            def edge_key_transposes(g):
                pe.wait_ge(keys_ready, g + 1)
                if g >= 1:
                    pe.wait_ge(skey_copied, g)
                    pe.wait_ge(lkey_copied, g)
                for bank, key in ((4, sc_f), (5, lk_f)):
                    for t in range(NS):
                        last = nc.tensor.transpose(ps[:, bank, t * P:t * P + BG], key[0:BG, g, t * P:(t + 1) * P],
                                                   ident[0:BG, 0:BG])
                last.then_inc(keyT_ready, 1)

            edge_key_transposes(0)
            edge_key_transposes(1)
            for j in range(NT):
                pe.wait_ge(x_normed, CHUNKS[j][-1][0] + 1)
                if j >= 2:
                    pe.wait_ge(h0_ready, j - 1)
                for k, rows in CHUNKS[j]:
                    last = nc.tensor.transpose(ps[:, 2 + j % 2, (k % TQ) * P:(k % TQ) * P + rows], xs[0:rows, k, :],
                                               ident[0:rows, 0:rows])
                last.then_inc(xT_ready, 1)
            for g in range(2, NG):
                edge_key_transposes(g)
            pe.wait_ge(nval_ready, 1)
            nc.tensor.matmul(psX[0:1, 0:1], nval[0:BG, 0:1], onecol[0:BG, 0:1], start=True, stop=True
                             ).then_inc(nval_summed, 1)
            pe.wait_ge(wT_copied, 4)
            pe.wait_ge(h0_ready, NT)
            pe.wait_ge(skey_copied, NG)
            pe.wait_ge(lkey_copied, NG)

            def count_blocks(b, ready, free):
                pe.wait_ge(onehots_ready, ready)
                if free is not None:
                    pe.wait_ge(counts_staged, free)
                for i in range(SIZES[b]):
                    for t in range(NS):
                        last = nc.tensor.matmul(blkps[SLOT[b]][:, i, 0:RL], ohS[SLOT[b]][:, i * NS + t, :],
                                                ohL[SLOT[b]][:, i * NS + t, 0:RL], start=(t == 0), stop=(t == NS - 1),
                                                skip_group_check=True)
                last.then_inc(blocks_done, 1)

            def count_group(g, beside=lambda b: None):
                for b in range(BPG):
                    if isinstance(g, int) and g == 0:
                        count_blocks(b, 2 * (b + 1), b - 3 if b >= 4 else None)
                    else:
                        count_blocks(b, g * (2 * BPG) + 2 * (b + 1), g * BPG + (b - PRIOR[b] + 1))
                    beside(b)

            def first_messages(g):
                def beside(b):
                    i = g * BPG + b
                    j = i // 2
                    if i % 2 == 0 and j >= 3:
                        pe.wait_ge(msg_lo, j - 2)
                    two = [c for c in CHUNKS[j] if c[0] in (2 * i, 2 * i + 1)]
                    if two:
                        last = node_product(two, init_bank[j])
                        if two[-1] == CHUNKS[j][-1]:
                            last.then_inc(msg_done, 1)
                return beside

            EARLY_SUMS = [(part, j) for part in range(2) for j in range(EARLY)]

            def sum_chunk(k, which, start=False):
                for part, j in which:
                    last = nc.tensor.matmul(acc0[j], msgs[:, bass.ds(mpart(0, k, part), H)],
                                            adj[:, bass.ds(k * RS + TW * j, TW)], start=start and part == 0,
                                            stop=False, skip_group_check=True)
                if which[-1] == EARLY_SUMS[-1]:
                    last.then_inc(chunk_summed, 1)

            def early_sums(k, start=False):
                def beside(b):
                    if b == 0:
                        pe.wait_ge(adj_loaded, 16 * k + 16)
                    sum_chunk(k, EARLY_SUMS[b:b + 1] if b < BPG - 1 else EARLY_SUMS[b:], start)
                return beside

            count_group(0, first_messages(0))
            count_group(1, first_messages(1))
            with pe.Fori(2, LAG) as g:
                count_group(g)
            pe.wait_ge(flag_ready, 1)
            pe.wait_ge(msg_lo, NT)
            count_group(LAG, early_sums(0, start=True))
            with pe.Fori(LAG + 1, NGRP) as g:
                count_group(g, early_sums(g - LAG))
            pe.wait_ge(counts_staged, NGRP * BPG)
            for k in range(NGRP - LAG):
                for part in range(2):
                    nc.tensor.matmul(acc0[EARLY], msgs[:, mpart(0, k, part):mpart(0, k, part) + H],
                                     adj[:, k * RS + TW * EARLY:k * RS + TW * (EARLY + 1)],
                                     start=(k == 0 and part == 0), stop=False, skip_group_check=True)
            for k in range(NGRP - LAG, NCH - LATE):
                pe.wait_ge(adj_loaded, 16 * (k + 1))
                sum_chunk(k, EARLY_SUMS)
            fast = pe.value_load(flag[0:1, 0:1], min_val=0, max_val=1)

            def gru_products(g, j, src_agg):
                w = WIDTH[j]
                h = hT[:, TW * j:TW * j + w]
                pe.wait_ge(r_ready, past(g))
                nc.tensor.matmul(psR[:, 0:w], WhhT[:, 0, :], h, start=True, stop=False)
                nc.tensor.matmul(psR[:, 0:w], WihT[:, 0, :], src_agg, start=False, stop=True).then_inc(r_summed, 1)
                pe.wait_ge(n_arg, past(g))
                nc.tensor.matmul(psH[:, 0:w], WhhT[:, 2, :], h, start=True, stop=True)
                nc.tensor.matmul(psI[:, 0:w], WihT[:, 2, :], src_agg, start=True, stop=True).then_inc(n_summed, 1)
                pe.wait_ge(z_ready, past(g))
                nc.tensor.matmul(psZ[:, 0:w], WhhT[:, 1, :], h, start=True, stop=False)
                nc.tensor.matmul(psZ[:, 0:w], WihT[:, 1, :], src_agg, start=False, stop=True).then_inc(z_summed, 1)

            def out_transpose(j):
                for k, rows in CHUNKS[j]:
                    last = nc.tensor.transpose(psM[0:rows, (k % TQ) * H:(k % TQ + 1) * H], hT[:, P * k:P * k + rows],
                                               ident[:, :])
                last.then_inc(outT_done, 1)

            with pe.If(fast):
                def messages(m, j):
                    pe.wait_ge(msg_hi, m)
                    pe.wait_ge(msg_lo, m)
                    node_product(CHUNKS[j]).then_inc(msg_done, 1)

                def next_messages(j):
                    if j >= 2:
                        pe.wait_ge(msg_hi, NT + j - 1)
                        pe.wait_ge(msg_lo, NT + j - 1)
                    node_product(CHUNKS[j], next_bank[j]).then_inc(msg_done, 1)

                def aggregate(j, k0, k1, waits={}, bank=None):
                    w = WIDTH[j]
                    bank = psAgg[j % 2] if bank is None else bank
                    for k in range(k0, k1):
                        if k in waits:
                            pe.wait_ge(msg_lo, waits[k])
                        for part in range(2):
                            last = nc.tensor.matmul(bank[:, 0:w], msgs[:, mpart(0, k, part):mpart(0, k, part) + H],
                                                    adj[:, k * RS + TW * j:k * RS + TW * j + w],
                                                    start=(k == 0 and part == 0), stop=(k == NCH - 1 and part == 1))
                    if k1 == NCH:
                        last.then_inc(agg_done, 1)

                def gru(g, j):
                    pe.wait_ge(aggT_ready, past(g + 1))
                    gru_products(g, j, aggT[:, 0:WIDTH[j]])

                def first_step():
                    def complete(j, k0=NCH - LATE):
                        for k in range(k0, NCH):
                            if j == FIRST[0] and k >= NCH - LATE:
                                pe.wait_ge(late_loaded[k - NCH], 16)
                            for part in range(2):
                                last = nc.tensor.matmul(acc0[j], msgs[:, mpart(0, k, part):mpart(0, k, part) + H],
                                                        adj[:, k * RS + TW * j:k * RS + TW * (j + 1)], start=False,
                                                        stop=(k == NCH - 1 and part == 1), skip_group_check=True)
                        last.then_inc(agg_done, 1)

                    complete(FIRST[0], NGRP - LAG)
                    complete(FIRST[1])
                    gru(0, FIRST[0])
                    for j in FIRST[2:EARLY + 1]:
                        complete(j)
                    t5 = NT - 2
                    gru(1, FIRST[1])
                    aggregate(t5, 0, 8, bank=acc0[t5])
                    gru(2, FIRST[2])
                    aggregate(t5, 8, 16, bank=acc0[t5])
                    gru(3, FIRST[3])
                    aggregate(t5, 16, 20, bank=acc0[t5])
                    pe.wait_ge(h_ready, past(2))
                    next_messages(0)
                    gru(4, FIRST[4])
                    pe.wait_ge(h_ready, past(3))
                    next_messages(1)
                    aggregate(t5, 20, NCH, bank=acc0[t5])
                    aggregate(NT - 1, 0, NCH, bank=acc0[NT - 1])
                    pe.wait_ge(h_ready, past(4))
                    next_messages(2)
                    pe.wait_ge(h_ready, past(5))
                    next_messages(3)
                    gru(5, t5)
                    next_messages(4)

                def step(s, last):
                    g0 = s * NT
                    waits = {TQ * j: g0 + j + 1 for j in range(EARLY, NT)}
                    pe.wait_ge(aggT_ready, past(g0))
                    pe.wait_ge(msgs_moved, s)
                    aggregate(0, 0, 6, waits)
                    gru(g0 - 1, NT - 1)
                    aggregate(0, 6, 14, waits)
                    pe.wait_ge(h_ready, past(g0 - 1))
                    messages(g0 + NT - 2, NT - 2)
                    aggregate(0, 14, 18, waits)
                    pe.wait_ge(h_ready, past(g0))
                    messages(g0 + NT - 1, NT - 1)
                    aggregate(0, 18, NCH, waits)
                    for j in range(NT):
                        if j < NT - 1:
                            if j >= 1:
                                pe.wait_ge(aggT_ready, past(g0 + j))
                            aggregate(j + 1, 0, NCH)
                        if last or j < NT - 1:
                            gru(g0 + j, j)
                        if 1 <= j < NT - 1:
                            pe.wait_ge(h_ready, past(g0 + j))
                            if last:
                                if j >= 2:
                                    pe.wait_ge(out_added, j - 1)
                                out_transpose(j - 1)
                            else:
                                messages(g0 + NT + j - 1, j - 1)

                first_step()
                with pe.Fori(1, STEPS - 1) as s:
                    step(s, False)
                step(STEPS - 1, True)
                for j in range(NT - 2, NT):
                    pe.wait_ge(h_ready, past(NT * (STEPS - 1) + j + 1))
                    pe.wait_ge(out_added, j)
                    out_transpose(j)
            with pe.Else():
                with pe.Fori(0, STEPS) as s:
                    pe.wait_ge(h_ready, past(s * NT))
                    for j in range(NT):
                        pe.wait_ge(g_node_ready, past(s * NT + j))
                        node_product(CHUNKS[j]).then_inc(g_node_sum, 1)
                    pe.wait_ge(g_node_ready, past(s * NT + NT))

                    def edges(u, i, first=False, final=False):
                        pe.wait_ge(g_gathered[i], s * (16 * ET // UN) + 16 * u + 16)
                        pe.wait_ge(g_onehot, s * ET + u * UN + (i + 1))
                        for j in range(NT):
                            last = nc.tensor.matmul(ps[:, j, 0:WIDTH[j]], g_msg[0:125, :],
                                                    g_one[0:125, TW * j:TW * j + WIDTH[j]], start=first, stop=final,
                                                    skip_group_check=True)
                            if final:
                                last.then_inc(agg_done, 1)
                        if not final:
                            last.then_inc(g_tile_done, 1)

                    for i in range(UN):
                        edges(0, i, first=(i == 0))
                    with pe.Fori(1, ET // UN - 1) as u:
                        for i in range(UN):
                            edges(u, i)
                    for i in range(UN):
                        edges(ET // UN - 1, i, final=(i == UN - 1))
                    pe.wait_ge(g_copied, NT * (s + 1))
                    pe.sem_inc(g_tile_done, 1)
                    for j in range(NT):
                        gru_products(s * NT + j, j, g_agg[:, TW * j:TW * j + WIDTH[j]])
                pe.wait_ge(h_ready, past(STEPS * NT))
                for j in range(NT):
                    if j >= 1:
                        pe.wait_ge(out_added, j)
                    out_transpose(j)


_INS = ['x', 'src', 'dst', 'L0_gnn_W_msg', 'L0_gnn_b_msg', 'L0_gnn_W_ih', 'L0_gnn_W_hh', 'L0_gnn_b_ih', 'L0_gnn_b_hh']
_OUTS = [((3125, 128), 'float32')]


def kernel(**inputs):
    import numpy as _np
    import concourse.bacc as _bacc
    from concourse import mybir as _mybir
    from concourse.bass_utils import run_bass_kernel_spmd as _run

    nc = _bacc.Bacc("TRN2", target_bir_lowering=False, num_devices=1)
    arrays, args = {}, []
    for name in _INS:
        a = _np.ascontiguousarray(inputs[name])
        arrays[f"in_{name}_dram"] = a
        args.append(nc.dram_tensor(f"in_{name}_dram", a.shape, _mybir.dt.from_np(a.dtype), kind="ExternalInput").ap())
    for i, (shape, dtype) in enumerate(_OUTS):
        dt = _mybir.dt.from_np(_np.dtype(dtype))
        args.append(nc.dram_tensor(f"out_{i}_dram", shape, dt, kind="ExternalOutput").ap())
    gnn_gated_recurrent_kernel(nc, *args)
    r = _run(nc, [arrays], core_ids=[0])
    got = tuple(r.results[0][f"out_{i}_dram"] for i in range(len(_OUTS)))
    return got[0]
```
